# Optimizing a Trainium2 kernel written in Bass

```python
import numpy as np
import jax
import jax.numpy as jnp

def _softmax(x, axis=-1):
    return jax.nn.softmax(x, axis=axis)

def _gelu(x):
    return jax.nn.gelu(x, approximate=True)

def _silu(x):
    return jax.nn.silu(x)

def _sigmoid(x):
    return jax.nn.sigmoid(x)

def _layernorm(x, axis=-1, eps=1e-05):
    m = jnp.mean(x, axis=axis, keepdims=True)
    v = jnp.var(x, axis=axis, keepdims=True)
    return (x - m) / jnp.sqrt(v + eps)

def _scatter_add(tgt, idx, src, axis=0):
    return tgt.at[idx].add(src)

def _segment_sum(src, seg, n):
    return jax.ops.segment_sum(src, seg, n)
kernel_name = 'mk_adaln_d2_jaxref_r8_752c05'

def setup_inputs(seed: int=0):
    np.random.seed(seed)
    _w = jnp.asarray

    def _L0_attn_setup():
        import jax, jax.numpy as jnp
        import numpy as np
        D_MODEL = 128
        HEADDIM = 64
        EXPAND = 2
        D_STATE = 128
        D_CONV = 4
        NGROUPS = 1
        D_INNER = EXPAND * D_MODEL
        NHEADS = D_INNER // HEADDIM
        CONV_DIM = D_INNER + 2 * NGROUPS * D_STATE
        D_IN_PROJ = 2 * D_INNER + 2 * NGROUPS * D_STATE + NHEADS
        BATCH = 2
        SEQLEN = 128
        EPS = 1e-05

        def silu(v):
            return v * jax.nn.sigmoid(v)

        def _mamba2(x, in_proj_w, conv_w, conv_b, dt_bias, A_log, D, norm_w, out_proj_w):
            b, l, _ = x.shape
            zxbcdt = x @ in_proj_w.T
            z, xBC, dt = jnp.split(zxbcdt, [D_INNER, D_INNER + CONV_DIM], axis=-1)
            dt = jax.nn.softplus(dt + dt_bias)
            rhs = conv_w.T[:, None, :]
            xBC = jax.lax.conv_general_dilated(xBC, rhs, window_strides=(1,), padding=[(D_CONV - 1, 0)], dimension_numbers=('NWC', 'WIO', 'NWC'), feature_group_count=CONV_DIM)
            xBC = silu(xBC + conv_b)
            xs, Bm, Cm = jnp.split(xBC, [D_INNER, D_INNER + D_STATE], axis=-1)
            xs = xs.reshape(b, l, NHEADS, HEADDIM)
            A = -jnp.exp(A_log)
            dA = jnp.exp(dt * A)

            def step(h, inp):
                dA_t, x_t, B_t, dt_t, C_t = inp
                h = h * dA_t[:, :, None, None] + jnp.einsum('bh,bhp,bn->bhpn', dt_t, x_t, B_t)
                y = jnp.einsum('bhpn,bn->bhp', h, C_t)
                return (h, y)
            h0 = jnp.zeros((b, NHEADS, HEADDIM, D_STATE), x.dtype)
            xs_t = xs.transpose(1, 0, 2, 3)
            _, ys = jax.lax.scan(step, h0, (dA.transpose(1, 0, 2), xs_t, Bm.transpose(1, 0, 2), dt.transpose(1, 0, 2), Cm.transpose(1, 0, 2)))
            y = ys.transpose(1, 0, 2, 3) + D[None, None, :, None] * xs
            y = y.reshape(b, l, D_INNER)
            y = y * silu(z)
            y = y * jax.lax.rsqrt(jnp.mean(y * y, axis=-1, keepdims=True) + EPS) * norm_w
            return y @ out_proj_w.T
        key = jax.random.key(seed)
        ks = jax.random.split(key, 8)
        s = 0.02
        return {'x': jax.random.normal(ks[0], (BATCH, SEQLEN, D_MODEL), jnp.float32), 'in_proj_w': jax.random.normal(ks[1], (D_IN_PROJ, D_MODEL), jnp.float32) * s, 'conv_w': jax.random.normal(ks[2], (CONV_DIM, D_CONV), jnp.float32) * 0.2, 'conv_b': jax.random.normal(ks[3], (CONV_DIM,), jnp.float32) * 0.02, 'dt_bias': jax.random.normal(ks[4], (NHEADS,), jnp.float32) * 0.1, 'A_log': jax.random.normal(ks[5], (NHEADS,), jnp.float32) * 0.5, 'D': jax.random.normal(ks[6], (NHEADS,), jnp.float32) * 0.5, 'norm_w': jnp.ones((D_INNER,), jnp.float32), 'out_proj_w': jax.random.normal(ks[7], (D_MODEL, D_INNER), jnp.float32) * s}
    _L0_attn_in = _L0_attn_setup()

    def _L0_ffn_setup():
        import jax, jax.numpy as jnp
        import numpy as np
        HIDDEN = 128
        NUM_EXPERTS = 8
        CAPACITY_FACTOR = 1.25
        key = jax.random.key(seed)
        k_tok, k_g, k_w1, k_b1, k_w2, k_b2 = jax.random.split(key, 6)
        B, S, H, E = (4, 256, HIDDEN, NUM_EXPERTS)
        tokens = jax.random.normal(k_tok, (B, S, H), dtype=jnp.float32)
        gate_w = jax.random.normal(k_g, (E, H), dtype=jnp.float32) * 0.02
        W1 = jax.random.normal(k_w1, (E, H, H), dtype=jnp.float32) * 0.02
        b1 = jax.random.normal(k_b1, (E, H), dtype=jnp.float32) * 0.02
        W2 = jax.random.normal(k_w2, (E, H, H), dtype=jnp.float32) * 0.02
        b2 = jax.random.normal(k_b2, (E, H), dtype=jnp.float32) * 0.02
        return {'tokens': tokens, 'gate_w': gate_w, 'W1': W1, 'b1': b1, 'W2': W2, 'b2': b2}
    _L0_ffn_in = _L0_ffn_setup()
    _L0_c = _w((lambda *s: np.random.randn(*s).astype(np.float32) * 0.05)(8, 128))
    _L0_wmod = _w((lambda *s: np.random.randn(*s).astype(np.float32) * 0.05)(128, 6 * 128) * 128 ** (-0.5))

    def _L1_attn_setup():
        import jax, jax.numpy as jnp
        import numpy as np
        HIDDEN = 128
        D_COMPLEX = HIDDEN // 2
        key = jax.random.key(seed)
        ks = jax.random.split(key, 9)
        B, S, H = (4, 512, HIDDEN)
        scale = 1.0 / np.sqrt(H)
        inp = {'x': jax.random.normal(ks[0], (B, S, H), dtype=jnp.float32), 'Wq': jax.random.normal(ks[1], (H, H), dtype=jnp.float32) * scale, 'bq': jnp.zeros((H,), dtype=jnp.float32), 'Wk': jax.random.normal(ks[2], (H, H), dtype=jnp.float32) * scale, 'bk': jnp.zeros((H,), dtype=jnp.float32), 'Wv': jax.random.normal(ks[3], (H, H), dtype=jnp.float32) * scale, 'bv': jnp.zeros((H,), dtype=jnp.float32), 'Wo': jax.random.normal(ks[4], (H, H), dtype=jnp.float32) * scale, 'bo': jnp.zeros((H,), dtype=jnp.float32)}
        return inp
    _L1_attn_in = _L1_attn_setup()

    def _L1_ffn_setup():
        import jax, jax.numpy as jnp
        import numpy as np
        B, S, D, F, E = (2, 256, 128, 512, 8)
        LN_EPS = 1e-05

        def _layer_norm(x, gamma, beta):
            mu = jnp.mean(x, axis=-1, keepdims=True)
            var = jnp.mean(jnp.square(x - mu), axis=-1, keepdims=True)
            return (x - mu) * jax.lax.rsqrt(var + LN_EPS) * gamma + beta
        key = jax.random.key(seed)
        ks = jax.random.split(key, 8)

        def xavier(k, shape):
            fan_in, fan_out = (shape[-1], shape[-2])
            a = jnp.sqrt(6.0 / (fan_in + fan_out))
            return jax.random.uniform(k, shape, jnp.float32, -a, a)
        return {'tgt': jax.random.normal(ks[0], (B, S, D), jnp.float32), 'Wr': xavier(ks[1], (E, D)), 'br': jnp.zeros((E,), jnp.float32), 'W1': xavier(ks[2], (E, F, D)), 'b1': jnp.zeros((E, F), jnp.float32), 'W2': xavier(ks[3], (E, D, F)), 'b2': jnp.zeros((E, D), jnp.float32), 'gamma': jnp.ones((D,), jnp.float32), 'beta': jnp.zeros((D,), jnp.float32)}
    _L1_ffn_in = _L1_ffn_setup()
    _L1_c = _w((lambda *s: np.random.randn(*s).astype(np.float32) * 0.05)(8, 128))
    _L1_wmod = _w((lambda *s: np.random.randn(*s).astype(np.float32) * 0.05)(128, 6 * 128) * 128 ** (-0.5))
    _d = {'L0_attn_x': _L0_attn_in['x'], 'L0_attn_in_proj_w': _L0_attn_in['in_proj_w'], 'L0_attn_conv_w': _L0_attn_in['conv_w'], 'L0_attn_conv_b': _L0_attn_in['conv_b'], 'L0_attn_dt_bias': _L0_attn_in['dt_bias'], 'L0_attn_A_log': _L0_attn_in['A_log'], 'L0_attn_D': _L0_attn_in['D'], 'L0_attn_norm_w': _L0_attn_in['norm_w'], 'L0_attn_out_proj_w': _L0_attn_in['out_proj_w'], 'L0_ffn_gate_w': _L0_ffn_in['gate_w'], 'L0_ffn_W1': _L0_ffn_in['W1'], 'L0_ffn_b1': _L0_ffn_in['b1'], 'L0_ffn_W2': _L0_ffn_in['W2'], 'L0_ffn_b2': _L0_ffn_in['b2'], 'L0_c': _L0_c, 'L0_wmod': _L0_wmod, 'L1_attn_Wq': _L1_attn_in['Wq'], 'L1_attn_bq': _L1_attn_in['bq'], 'L1_attn_Wk': _L1_attn_in['Wk'], 'L1_attn_bk': _L1_attn_in['bk'], 'L1_attn_Wv': _L1_attn_in['Wv'], 'L1_attn_bv': _L1_attn_in['bv'], 'L1_attn_Wo': _L1_attn_in['Wo'], 'L1_attn_bo': _L1_attn_in['bo'], 'L1_ffn_Wr': _L1_ffn_in['Wr'], 'L1_ffn_br': _L1_ffn_in['br'], 'L1_ffn_W1': _L1_ffn_in['W1'], 'L1_ffn_b1': _L1_ffn_in['b1'], 'L1_ffn_W2': _L1_ffn_in['W2'], 'L1_ffn_b2': _L1_ffn_in['b2'], 'L1_ffn_gamma': _L1_ffn_in['gamma'], 'L1_ffn_beta': _L1_ffn_in['beta'], 'L1_c': _L1_c, 'L1_wmod': _L1_wmod}
    _x0 = _d['L0_attn_x']
    _d['L0_attn_x'] = jax.random.normal(jax.random.fold_in(jax.random.key(seed), 1), (8, 512, 128), dtype=_x0.dtype)
    del _x0
    return _d

def reference(L0_attn_x, L0_attn_in_proj_w, L0_attn_conv_w, L0_attn_conv_b, L0_attn_dt_bias, L0_attn_A_log, L0_attn_D, L0_attn_norm_w, L0_attn_out_proj_w, L0_ffn_gate_w, L0_ffn_W1, L0_ffn_b1, L0_ffn_W2, L0_ffn_b2, L0_c, L0_wmod, L1_attn_Wq, L1_attn_bq, L1_attn_Wk, L1_attn_bk, L1_attn_Wv, L1_attn_bv, L1_attn_Wo, L1_attn_bo, L1_ffn_Wr, L1_ffn_br, L1_ffn_W1, L1_ffn_b1, L1_ffn_W2, L1_ffn_b2, L1_ffn_gamma, L1_ffn_beta, L1_c, L1_wmod):

    def _L0_attn_ref(x, in_proj_w, conv_w, conv_b, dt_bias, A_log, D, norm_w, out_proj_w):
        import jax, jax.numpy as jnp
        import numpy as np
        D_MODEL = 128
        HEADDIM = 64
        EXPAND = 2
        D_STATE = 128
        D_CONV = 4
        NGROUPS = 1
        D_INNER = EXPAND * D_MODEL
        NHEADS = D_INNER // HEADDIM
        CONV_DIM = D_INNER + 2 * NGROUPS * D_STATE
        D_IN_PROJ = 2 * D_INNER + 2 * NGROUPS * D_STATE + NHEADS
        BATCH = 2
        SEQLEN = 128
        EPS = 1e-05

        def silu(v):
            return v * jax.nn.sigmoid(v)

        def _mamba2(x, in_proj_w, conv_w, conv_b, dt_bias, A_log, D, norm_w, out_proj_w):
            b, l, _ = x.shape
            zxbcdt = x @ in_proj_w.T
            z, xBC, dt = jnp.split(zxbcdt, [D_INNER, D_INNER + CONV_DIM], axis=-1)
            dt = jax.nn.softplus(dt + dt_bias)
            rhs = conv_w.T[:, None, :]
            xBC = jax.lax.conv_general_dilated(xBC, rhs, window_strides=(1,), padding=[(D_CONV - 1, 0)], dimension_numbers=('NWC', 'WIO', 'NWC'), feature_group_count=CONV_DIM)
            xBC = silu(xBC + conv_b)
            xs, Bm, Cm = jnp.split(xBC, [D_INNER, D_INNER + D_STATE], axis=-1)
            xs = xs.reshape(b, l, NHEADS, HEADDIM)
            A = -jnp.exp(A_log)
            dA = jnp.exp(dt * A)

            def step(h, inp):
                dA_t, x_t, B_t, dt_t, C_t = inp
                h = h * dA_t[:, :, None, None] + jnp.einsum('bh,bhp,bn->bhpn', dt_t, x_t, B_t)
                y = jnp.einsum('bhpn,bn->bhp', h, C_t)
                return (h, y)
            h0 = jnp.zeros((b, NHEADS, HEADDIM, D_STATE), x.dtype)
            xs_t = xs.transpose(1, 0, 2, 3)
            _, ys = jax.lax.scan(step, h0, (dA.transpose(1, 0, 2), xs_t, Bm.transpose(1, 0, 2), dt.transpose(1, 0, 2), Cm.transpose(1, 0, 2)))
            y = ys.transpose(1, 0, 2, 3) + D[None, None, :, None] * xs
            y = y.reshape(b, l, D_INNER)
            y = y * silu(z)
            y = y * jax.lax.rsqrt(jnp.mean(y * y, axis=-1, keepdims=True) + EPS) * norm_w
            return y @ out_proj_w.T
        return x + _mamba2(x, in_proj_w, conv_w, conv_b, dt_bias, A_log, D, norm_w, out_proj_w)

    def _L0_ffn_ref(tokens, gate_w, W1, b1, W2, b2):
        import jax, jax.numpy as jnp
        import numpy as np
        HIDDEN = 128
        NUM_EXPERTS = 8
        CAPACITY_FACTOR = 1.25
        B, S, H = tokens.shape
        E = gate_w.shape[0]
        T = B * S
        x = tokens.reshape(T, H)
        logits = x @ gate_w.T
        probs = jax.nn.softmax(logits, axis=-1)
        top2_w, top2_idx = jax.lax.top_k(probs, 2)
        cap = int(CAPACITY_FACTOR * T / E)
        counts = jnp.bincount(top2_idx.reshape(-1), length=E)
        keep = (counts <= cap).astype(x.dtype)
        comb = jnp.zeros((T, E), dtype=x.dtype).at[jnp.arange(T)[:, None], top2_idx].add(top2_w)
        comb = comb * keep[None, :]
        h = jax.nn.relu(jnp.einsum('th,ehf->tef', x, W1) + b1[None, :, :])
        y = jnp.einsum('teh,ehf->tef', h, W2) + b2[None, :, :]
        out = jnp.einsum('te,tef->tf', comb, y)
        return out.reshape(B, S, H)

    def _L1_attn_ref(x, Wq, bq, Wk, bk, Wv, bv, Wo, bo):
        import jax, jax.numpy as jnp
        import numpy as np
        HIDDEN = 128
        D_COMPLEX = HIDDEN // 2
        Q = x @ Wq.T + bq
        K = x @ Wk.T + bk
        V = x @ Wv.T + bv
        scores = jnp.einsum('bqd,bkd->bqk', Q, K) / np.sqrt(D_COMPLEX)
        weights = jax.nn.softmax(scores, axis=-1)
        out = jnp.einsum('bqk,bkd->bqd', weights, V)
        return out @ Wo.T + bo

    def _L1_ffn_ref(tgt, Wr, br, W1, b1, W2, b2, gamma, beta):
        import jax, jax.numpy as jnp
        import numpy as np
        B, S, D, F, E = (2, 256, 128, 512, 8)
        LN_EPS = 1e-05

        def _layer_norm(x, gamma, beta):
            mu = jnp.mean(x, axis=-1, keepdims=True)
            var = jnp.mean(jnp.square(x - mu), axis=-1, keepdims=True)
            return (x - mu) * jax.lax.rsqrt(var + LN_EPS) * gamma + beta
        logits = jnp.einsum('bsd,ed->bse', tgt, Wr) + br
        top_v, top_i = jax.lax.top_k(logits, 2)
        top_w = jax.nn.softmax(top_v, axis=-1)
        n_exp = logits.shape[-1]
        router_w = jnp.sum(jax.nn.one_hot(top_i, n_exp, dtype=top_w.dtype) * top_w[..., None], axis=-2)
        h = jnp.einsum('bsd,efd->bsef', tgt, W1) + b1
        h = jax.nn.relu(h)
        o = jnp.einsum('bsef,edf->bsed', h, W2) + b2
        tgt2 = jnp.einsum('bsed,bse->bsd', o, router_w)
        return _layer_norm(tgt + tgt2, gamma, beta)
    x = L0_attn_x
    mod = (_silu(L0_c) @ L0_wmod).reshape(L0_c.shape[0], 6, 1, -1)
    sa, ca, ga, sb, cb, gb = (mod[:, 0], mod[:, 1], mod[:, 2], mod[:, 3], mod[:, 4], mod[:, 5])
    ga = (2 * (ga >= 0) - 1) * jnp.maximum(jnp.abs(ga), 0.25)
    gb = (2 * (gb >= 0) - 1) * jnp.maximum(jnp.abs(gb), 0.25)
    h = _layernorm(x, axis=-1) * (1 + ca) + sa
    x = x + ga * _L0_attn_ref(h, L0_attn_in_proj_w, L0_attn_conv_w, L0_attn_conv_b, L0_attn_dt_bias, L0_attn_A_log, L0_attn_D, L0_attn_norm_w, L0_attn_out_proj_w)
    h = _layernorm(x, axis=-1) * (1 + cb) + sb
    x = x + gb * _L0_ffn_ref(h, L0_ffn_gate_w, L0_ffn_W1, L0_ffn_b1, L0_ffn_W2, L0_ffn_b2)
    mod = (_silu(L1_c) @ L1_wmod).reshape(L1_c.shape[0], 6, 1, -1)
    sa, ca, ga, sb, cb, gb = (mod[:, 0], mod[:, 1], mod[:, 2], mod[:, 3], mod[:, 4], mod[:, 5])
    ga = (2 * (ga >= 0) - 1) * jnp.maximum(jnp.abs(ga), 0.25)
    gb = (2 * (gb >= 0) - 1) * jnp.maximum(jnp.abs(gb), 0.25)
    h = _layernorm(x, axis=-1) * (1 + ca) + sa
    x = x + ga * _L1_attn_ref(h, L1_attn_Wq, L1_attn_bq, L1_attn_Wk, L1_attn_bk, L1_attn_Wv, L1_attn_bv, L1_attn_Wo, L1_attn_bo)
    h = _layernorm(x, axis=-1) * (1 + cb) + sb
    x = x + gb * _L1_ffn_ref(h, L1_ffn_Wr, L1_ffn_br, L1_ffn_W1, L1_ffn_b1, L1_ffn_W2, L1_ffn_b2, L1_ffn_gamma, L1_ffn_beta)
    return x

_drawn_inputs = setup_inputs


def setup_inputs(seed=0):
    import zlib

    import numpy as np

    out = dict(_drawn_inputs(seed))
    spreads = {'L0_attn_norm_w': (1.0, 0.6),
     'L1_attn_bq': (0.0, 0.8),
     'L1_attn_bk': (0.0, 2.0),
     'L1_attn_bv': (0.0, 0.285),
     'L1_attn_bo': (0.0, 0.308),
     'L1_ffn_br': (0.0, 0.466),
     'L1_ffn_b1': (0.0, 0.532),
     'L1_ffn_b2': (0.0, 0.479),
     'L1_ffn_gamma': (1.0, 0.2),
     'L1_ffn_beta': (0.0, 0.344)}
    factors = {'L0_attn_conv_b': 5.583, 'L0_attn_dt_bias': 64.0, 'L0_attn_A_log': 64.0}
    for name, (base, spread) in spreads.items():
        noise = np.random.default_rng([zlib.crc32(name.encode()), seed]).standard_normal(out[name].shape)
        drawn = base * np.exp(spread * noise) if base else spread * noise
        out[name] = jnp.asarray(drawn.astype(out[name].dtype))
    for name, factor in factors.items():
        out[name] = (out[name] * factor).astype(out[name].dtype)
    return out
```

```python
from contextlib import ExitStack

import concourse.bass as bass
from concourse import mybir

P = 128
F32 = mybir.dt.float32
F32R = mybir.dt.float32r
I32 = mybir.dt.int32
U32 = mybir.dt.uint32
ALU = mybir.AluOpType
ACT = mybir.ActivationFunctionType
AX = mybir.AxisListType

NB = 8
SEQ = 512
NC = SEQ // P
NT = NB * NC
D = 128
DI = 256
NH = 4
HD = DI // NH
NTAP = 4
NE = 8
FF = 512
NG = FF // P
EPS = 1e-5
CAP = int(1.25 * NB * SEQ / NE)


class Chip:

    def __init__(self, nc, a, ctx):
        self.nc, self.a, self.ctx = nc, a, ctx
        self.bank = [ctx.enter_context(nc.psum_tensor(f"bank{i}", [P, 512], F32)) for i in range(8)]
        self.S = {}
        sb = lambda name, shape, dt=F32: ctx.enter_context(nc.sbuf_tensor(name, shape, dt))
        self.x = sb("x", [P, NT, D])
        self.h_all = sb("h_all", [P, NB, SEQ])
        self.ident = sb("ident", [P, P])
        self.ones = sb("ones", [P, P])
        self.half_neg = sb("half_neg", [P, NC])
        self.eps = sb("eps", [P, NC])
        self.mod = sb("mod", [P, 2, 6, NB])
        self.rows0 = sb("rows0", [P, NB, 3, D])
        self.gate_rows = sb("gate_rows", [P, 3, NB, D])
        self.lg = sb("lg", [P, NT, NE])
        self.ix = sb("ix", [P, NT, 2])
        self.iota = sb("iota", [P, NE])
        self.attn_w = sb("attn_w", [P, 4, D])
        self.attn_b = sb("attn_b", [P, 2])
        self.bv = sb("bv", [P, D])
        self.bo = sb("bo", [P, D])
        self.wr = sb("wr", [P, NE])
        self.br = sb("br", [P, NE])

    def sems(self, names):
        for n in names:
            self.S[n] = self.ctx.enter_context(self.nc.semaphore(n))

    def wait(self, e, name, n):
        if not isinstance(n, int) or n > 0:
            e.wait_ge(self.S[name], n)

    def alone(self, e, s):
        if not isinstance(s, int):
            e.nop(nofuse=True)


def bc3(ap, n, m):
    return ap.rearrange("p (h o) -> p h o", o=1).broadcast_to([P, n, m])


def conditioning(nc, k, a):
    x, ident, ones, mod, rows0, gate_rows = k.x, k.ident, k.ones, k.mod, k.rows0, k.gate_rows
    bank, S = k.bank, k.S
    k.sems(("c_in", "x_in", "aw_in", "c_tanh", "c_dve", "c_mm", "c_rows", "c_ev", "c_const"))
    with ExitStack() as ctx:
        sb = lambda name, shape, dt=F32: ctx.enter_context(nc.sbuf_tensor(name, shape, dt))
        cT = sb("cT", [P, 2 * NB])
        cu = sb("cu", [P, 2 * NB])
        cub = sb("cub", [P, 2 * NB, P])
        wmod = sb("wmod", [P, 2, 6 * D])
        gsg = sb("gsg", [P, 4 * NB * D])
        gab = sb("gab", [P, 4 * NB * D])
        block = ctx.enter_context(nc.Block())

        @block.sync
        def _(sp):
            for dst, key in ((cT, "cT"), (wmod, "wmod"), (ident, "ident")):
                sp.dma_start(dst[:], a[key]).then_inc(S["c_in"], 16)
            sp.dma_start(x[:], a["x"].rearrange("b (c p) d -> p (b c) d", p=P)).then_inc(S["x_in"], 16)
            for dst, key in ((k.attn_w, "attn_w"), (k.attn_b, "attn_b"), (k.bv, "bv"), (k.bo, "bo"), (k.wr, "wr"), (k.br, "br"), (k.iota, "iota")):
                sp.dma_start(dst[:], a[key]).then_inc(S["aw_in"], 16)
            sp.wait_ge(S["x_in"], 16)
            sp.wait_ge(S["aw_in"], 16 * 7)

        @block.gpsimd
        def _(pool):
            nc.gpsimd.memset(k.half_neg[:], -0.5)
            nc.gpsimd.memset(k.eps[:], EPS)
            nc.gpsimd.memset(ones[:], 1.0)

        @block.scalar
        def _(act):
            act.wait_ge(S["c_in"], 48)
            nc.scalar.activation(cu[:], cT[:], ACT.Tanh, scale=0.5).then_inc(S["c_tanh"], 1)
            for b in range(NB):
                act.wait_ge(S["c_rows"], b + 1)
                o = (b % 2) * 3
                nc.scalar.activation(rows0[:, b].rearrange("p k d -> p (k d)"), bank[1 + o][:, 0:3 * D], ACT.Copy)
                nc.scalar.activation(gate_rows[:, 0, b, :], bank[2 + o][:, 0:D], ACT.Copy)
                nc.scalar.activation(gate_rows[:, 1, b, :], bank[3 + o][:, 0:D], ACT.Copy)
                nc.scalar.activation(gate_rows[:, 2, b, :], bank[3 + o][:, D:2 * D], ACT.Copy).then_inc(S["c_ev"], 1)

        @block.vector
        def _(dve):
            v = nc.vector
            n = [0]

            def step(ins):
                n[0] += 1
                ins.then_inc(S["c_dve"], 1)
                dve.wait_ge(S["c_dve"], n[0])

            dve.wait_ge(S["c_in"], 48)
            dve.wait_ge(S["c_tanh"], 1)
            step(v.tensor_scalar(cT[:], cT[:], 0.5, None, ALU.mult))
            step(v.scalar_tensor_tensor(out=cu[:], in0=cu[:], scalar=1.0, in1=cT[:], op0=ALU.add, op1=ALU.mult))
            step(v.tensor_copy(cub[:], bc3(cu[:], 2 * NB, P)))
            dve.wait_ge(S["c_mm"], 1)
            step(v.tensor_copy(mod[:].rearrange("p l k b -> p (l k b)"), bank[0][:, 0:12 * NB]))
            for l in range(2):
                for i in (1, 4):
                    step(v.tensor_scalar(mod[:, l, i, :], mod[:, l, i, :], 1.0, None, ALU.add))

            def gate(g, w, s, b_):
                step(v.tensor_scalar(s, g, 0.0, 2.0, ALU.is_ge, ALU.mult))
                step(v.tensor_scalar(b_, g, -1.0, None, ALU.mult))
                step(v.tensor_tensor(b_, b_, g, ALU.max))
                step(v.tensor_scalar(b_, b_, 0.25, None, ALU.max))
                step(v.scalar_tensor_tensor(out=g, in0=s, scalar=1.0, in1=b_, op0=ALU.subtract, op1=ALU.mult))

            dve.wait_ge(S["c_ev"], NB)
            m = NB * D
            as3 = lambda t: t[:, 0:m].rearrange("p (b d) -> p b d", b=NB)
            gate(rows0[:, :, 2, :], m, as3(gsg), as3(gab))
            gate(gate_rows[:].rearrange("p k b d -> p (k b d)"), 3 * m, gsg[:, m:4 * m], gab[:, m:4 * m])
            step(v.tensor_scalar(rows0[:, :, 1, :], rows0[:, :, 1, :], 1.0, None, ALU.add))

        @block.tensor
        def _(pe):
            t_ = nc.tensor
            pe.wait_ge(S["c_in"], 48)
            pe.wait_ge(S["c_dve"], 2)
            for l in range(2):
                for i in range(6):
                    mm = t_.matmul(bank[0][:, (l * 6 + i) * NB:(l * 6 + i + 1) * NB], wmod[:, l, i * D:(i + 1) * D],
                                   cu[:, l * NB:(l + 1) * NB], start=True, stop=True)
            mm.then_inc(S["c_mm"], 1)
            pe.wait_ge(S["c_dve"], 3)
            for b in range(NB):
                if b >= 2:
                    pe.wait_ge(S["c_ev"], b - 1)
                o = (b % 2) * 3
                t_.matmul(bank[1 + o][:, 0:3 * D], cub[:, b, :], wmod[:, 0, 0:3 * D], start=True, stop=True)
                t_.matmul(bank[2 + o][:, 0:D], cub[:, b, :], wmod[:, 0, 5 * D:6 * D], start=True, stop=True)
                t_.matmul(bank[3 + o][:, 0:D], cub[:, NB + b, :], wmod[:, 1, 2 * D:3 * D], start=True, stop=True)
                t_.matmul(bank[3 + o][:, D:2 * D], cub[:, NB + b, :], wmod[:, 1, 5 * D:6 * D], start=True, stop=True).then_inc(S["c_rows"], 1)


def mixer(nc, chip, a):
    x, h_all, ident, mod, ones, lg, ix, rows0, bank, S = (
        chip.x, chip.h_all, chip.ident, chip.mod, chip.ones, chip.lg, chip.ix, chip.rows0, chip.bank, chip.S)
    half_neg, eps, wait, alone = chip.half_neg[:, 0:1], chip.eps[:, 0:1], chip.wait, chip.alone
    with ExitStack() as ctx:
        def sb(name, shape, dt=F32):
            return ctx.enter_context(nc.sbuf_tensor(name, shape, dt))

        wc_hi = sb("wc_hi", [P, NTAP, SEQ], F32R)
        wc_lo = sb("wc_lo", [P, NTAP, SEQ], F32R)
        wz = sb("wz", [P, DI + NH])
        wz_hi = sb("wz_hi", [P, DI + NH], F32R)
        wz_lo = sb("wz_lo", [P, DI + NH], F32R)
        conv_b = sb("conv_b", [P, 4])
        hconv_b = sb("hconv_b", [P, 4])
        dt_b = sb("dt_b", [P, NH])
        a_neg = sb("a_neg", [P, NC * NH])
        a_log = sb("a_log", [P, NC * NH])
        d_bc = sb("d_bc", [P, DI])
        norm_w = sb("norm_w", [P, 2])
        wo = sb("wo", [P, 2, D])
        wo8 = sb("wo8", [P, NB, 2, D])
        res_g = sb("res_g", [P, NB, D])
        res_b = sb("res_b", [P, NB, D])
        gw = sb("gw", [P, NE])
        ident4 = sb("ident4", [P, NC * P])
        sel = sb("sel", [16, 16 * P])
        sel127 = sb("sel127", [P, P])
        zero16 = sb("zero16", [16, P])

        st1 = sb("st1", [P, 2, 6]); mv1 = sb("mv1", [P, 2, 2]); ve1 = sb("ve1", [P, 2, 1]); rs1 = sb("rs1", [P, 2, 1])
        st2 = sb("st2", [P, 2, 6]); mv2 = sb("mv2", [P, 2, 2]); ve2 = sb("ve2", [P, 2, 1]); rs2 = sb("rs2", [P, 2, 1])
        xn1 = sb("xn1", [P, 2, D]); xn2 = sb("xn2", [P, 2, D])
        rt1 = sb("rt1", [P, 2, D]); rt2 = sb("rt2", [P, 2, D])
        h_new = sb("h_new", [P, SEQ])
        h_hi = sb("h_hi", [P, 4 + SEQ], F32R)
        h_lo = sb("h_lo", [P, 4 + SEQ], F32R)
        cv = sb("cv", [P, 2, 4, SEQ])
        ct = sb("ct", [P, 2, 4, SEQ])
        cwb, wstage = cv[:, 0], ct[:, 0]
        zu = sb("zu", [P, 2, DI]); zt = sb("zt", [P, 2, DI])
        zs = sb("zs", [P, 2, NC, DI])
        dtr = sb("dtr", [P, NC * NH]); dta = sb("dta", [P, NC * NH]); dte = sb("dte", [P, NC * NH]); dtl = sb("dtl", [P, NC * NH])
        dt = sb("dt", [P, 2, NC * NH]); dax = sb("dax", [P, NC * NH]); da = sb("da", [P, NC * NH])
        da_t = sb("da_t", [16, 2, P]); cum_t = sb("cum_t", [16, P])
        cum = sb("cum", [P, 2, NC * NH]); tot = sb("tot", [P, 2, NC * NH])
        xc = sb("xc", [P, 2, 4, P])
        xb = sb("xb", [P, 2, 3 * P])
        lt = sb("lt", [P, 2, 4 * P]); mt = sb("mt", [P, 2, 4 * P])
        xdt = sb("xdt", [P, 2, DI]); xdw = sb("xdw", [P, 2, DI]); xd = sb("xd", [P, 2, DI])
        state = sb("state", [P, DI]); state_d = sb("state_d", [P, DI])
        y1 = sb("y1", [P, DI]); y2 = sb("y2", [P, DI]); y3 = sb("y3", [P, DI])
        yz = sb("yz", [P, 2, DI]); ysq = sb("ysq", [P, DI]); ss = sb("ss", [P, 2, 1]); sse = sb("sse", [P, 2, 1]); rr = sb("rr", [P, 2, 1])
        yt = sb("yt", [P, 2, DI])
        hc = sb("hc", [P, 2, P])
        lgc = sb("lgc", [P, 2, NE]); mx = sb("mx", [P, 2, NE]); mi = sb("mi", [P, 2, NE], U32)

        chip.sems((
            "w_in", "set_pool", "set_dve", "set_act",
            "pe_slot", "act_slot", "dve_slot", "pool_slot",
            "ln1_stats", "ln1_mv", "ln1_ve", "ln1_rs", "ln1_xn", "res_1", "res_2", "h_staged", "h_split", "h_split_hi",
            "f_mm", "f_v", "f_t", "z_mm", "z_act", "z_dt", "z_s",
            "d_abs", "d_exp", "d_ln", "d_dt", "d_dta", "d_da", "d_tr", "d_tz", "d_scan", "d_tr2", "d_cum", "d_mm", "d_tot",
            "s_xc", "s_tr", "s_g", "s_bc", "s_xb", "s_lt", "s_mt", "s_xdt", "s_xdw", "s_xd",
            "s_ymm", "s_smm", "s_sd", "s_state", "s_y1", "s_y2", "s_y3", "s_yz", "s_ss", "s_sse", "s_rr",
            "t_mm", "t_h", "t_y", "t_h2", "o_mm", "o_x", "ln2_stats", "ln2_mv", "ln2_ve", "ln2_rs", "ln2_xn",
            "r_mm", "r_lg", "r_mx", "r_mi", "h_kept"))
        block = ctx.enter_context(nc.Block())

        DVE_SETUP, POOL_SETUP = 3, 29
        FIRST, LAST = -9, NT + 3

        def slots(e, body):
            for s in range(FIRST, NC):
                body(s, s // NC, s % NC, lambda lag: 0 <= s - lag < NT)
            with e.Fori(1, NB - 3) as b:
                for c in range(NC):
                    body(b * NC + c, b, c, lambda lag: True)
            for s in range((NB - 3) * NC, LAST):
                body(s, s // NC, s % NC, lambda lag: 0 <= s - lag < NT)

        def slot_begins(e, s):
            for name in ("pe_slot", "act_slot", "dve_slot", "pool_slot"):
                wait(e, name, s - 2 - FIRST + 1)

        def hv(ap):
            return ap.rearrange("p (h o) -> p h o", h=NH)

        def bc3(ap, n, m):
            return ap.rearrange("p (h o) -> p h o", o=1).broadcast_to([P, n, m])

        @block.sync
        def _(sp):
            for dst, key in ((wstage[:, 0, :], "w_xbc"), (cwb, "conv_w"), (wz[:], "w_zdt"), (conv_b[:], "conv_b"), (dt_b[:], "dt_b"),
                             (a_log[:], "a_log"), (d_bc[:], "d_bc"), (norm_w[:], "norm_w"), (wo[:], "w_out"),
                             (gw[:], "gate_w"), (ident4[:], "ident4"), (sel[:], "sel"), (sel127[:], "sel127")):
                sp.dma_start(dst, a[key]).then_inc(S["w_in"], 16)
            sp.wait_ge(S["w_in"], 16 * 13)

        @block.gpsimd
        def _(pool):
            g = nc.gpsimd
            n = [0]

            def step(ins):
                n[0] += 1
                ins.then_inc(S["set_pool"], 1)
                pool.wait_ge(S["set_pool"], n[0])

            step(g.memset(zero16[:], 0.0))
            step(g.memset(da_t[:, :, 0:1], 0.0))
            step(g.memset(h_hi[:, 0:4].bitcast(F32), 0.0))
            step(g.memset(h_lo[:, 0:4].bitcast(F32), 0.0))
            pool.wait_ge(S["w_in"], 16 * 13)
            for k in range(NTAP):
                step(g.tensor_tensor(cwb[:, k, :], cwb[:, k, :], wstage[:, 0, :], ALU.mult))
                step(g.tensor_copy(wc_hi[:, k, :], cwb[:, k, :]))
                step(g.tensor_tensor(wc_lo[:, k, :], cwb[:, k, :], wc_hi[:, k, :].bitcast(F32), ALU.subtract))
            step(g.tensor_copy(wz_hi[:], wz[:]))
            step(g.tensor_tensor(wz_lo[:], wz[:], wz_hi[:].bitcast(F32), ALU.subtract))
            step(g.tensor_scalar(hconv_b[:], conv_b[:], 0.5, None, ALU.mult))
            for k in range(2):
                step(g.tensor_scalar(wo[:, k, :], wo[:, k, :], norm_w[:, k:k + 1], None, ALU.mult))
            for b in range(NB):
                step(g.tensor_tensor(wo8[:, b], wo[:], rows0[:, b, 2, :].rearrange("p (o d) -> p o d", o=1).broadcast_to([P, 2, D]), ALU.mult))
            assert n[0] == POOL_SETUP, n[0]

            def body(s, b, c, has):
                slot_begins(pool, s)
                if has(-9):
                    t, p, ba = s + 9, (c + 1) % 2, b + 2 if c < 3 else b + 3
                    wait(pool, "ln1_mv", t + 1)
                    g.tensor_tensor(ve1[:, p, :], mv1[:, p, 1:2], eps, ALU.add).then_inc(S["ln1_ve"], 1)
                    wait(pool, "ln1_ve", t + 1)
                    g.tensor_tensor(rs1[:, p, :], ve1[:, p, :], half_neg, ALU.pow).then_inc(S["ln1_rs"], 1)
                if has(1):
                    cs = (c - 1) % 4
                    if cs in (1, 2):
                        wait(pool, "s_state", s - 1)
                        alone(pool, s)
                        q = b % 2
                        g.tensor_tensor(hv(state_d[:]), hv(state[:]),
                                        bc3(tot[:, q, cs * NH:cs * NH + NH], NH, HD), ALU.mult).then_inc(S["s_sd"], 1)
                    else:
                        pool.drain().then_inc(S["s_sd"], 1)
                if has(0):
                    p, q = c % 2, b % 2
                    wait(pool, "s_xb", s + 1)
                    wait(pool, "s_smm", s - 1)
                    wait(pool, "s_y3", s - 1)
                    g.tensor_tensor(xd[:, p, :], xb[:, p, 0:DI], d_bc[:], ALU.mult).then_inc(S["s_xd"], 1)
                    g.tensor_tensor(hv(xdt[:, p, :]), hv(xb[:, p, 0:DI]), bc3(dt[:, q, c * NH:c * NH + NH], NH, HD),
                                    ALU.mult).then_inc(S["s_xdt"], 1)
                    wait(pool, "s_xdt", s + 1)
                    wait(pool, "s_lt", s + 1)
                    g.tensor_tensor(hv(xdw[:, p, :]), hv(xdt[:, p, :]),
                                    lt[:, p, :].rearrange("p (h i) -> p h i", h=NH)[:, :, P - 1:P].broadcast_to([P, NH, HD]),
                                    ALU.mult).then_inc(S["s_xdw"], 1)
                if has(-9):
                    wait(pool, "ln1_xn", t + 1)
                    alone(pool, s)
                    g.tensor_tensor(rt1[:, (c + 1) % 2, :], xn1[:, (c + 1) % 2, :], res_g[:, ba, :], ALU.mult).then_inc(S["res_1"], 1)
                if has(2):
                    t2, p = s - 2, c % 2
                    wait(pool, "ln2_mv", t2 + 1)
                    g.tensor_tensor(ve2[:, p, :], mv2[:, p, 1:2], eps, ALU.add).then_inc(S["ln2_ve"], 1)
                    wait(pool, "ln2_ve", t2 + 1)
                    g.tensor_tensor(rs2[:, p, :], ve2[:, p, :], half_neg, ALU.pow).then_inc(S["ln2_rs"], 1)
                if has(-9):
                    wait(pool, "res_1", t + 1)
                    alone(pool, s)
                    g.tensor_tensor(rt2[:, (c + 1) % 2, :], rt1[:, (c + 1) % 2, :], res_b[:, ba, :], ALU.add).then_inc(S["res_2"], 1)
                if has(1):
                    t1, p = s - 1, (c + 1) % 2
                    wait(pool, "s_ss", t1 + 1)
                    wait(pool, "o_x", s - 2)
                    g.tensor_tensor(sse[:, p, :], ss[:, p, :], eps, ALU.add).then_inc(S["s_sse"], 1)
                    wait(pool, "s_sse", t1 + 1)
                    g.tensor_tensor(rr[:, p, :], sse[:, p, :], half_neg, ALU.pow).then_inc(S["s_rr"], 1)
                if has(-9):
                    wait(pool, "res_2", t + 1)
                    alone(pool, s)
                    g.tensor_tensor(x[:, t, :], x[:, t, :], rt2[:, (c + 1) % 2, :], ALU.add)
                if has(3):
                    t3, p = s - 3, (c + 1) % 2
                    bb = b if c == 3 else b - 1
                    cc = (c + 1) % 4
                    wait(pool, "t_h2", t3 + 1)
                    wait(pool, "r_lg", t3 + 1)
                    alone(pool, s)
                    g.tensor_copy(h_all[:, bb, cc * P:cc * P + P], hc[:, p, :])
                    g.tensor_copy(lg[:, t3, :], lgc[:, p, :])
                if has(-8) and c == 3:
                    wait(pool, "h_staged", s + 9)
                    wait(pool, "f_mm", s + 4 + 1)
                    alone(pool, s)
                    g.tensor_copy(h_hi[:, 3:3 + SEQ], h_new[:]).then_inc(S["h_split_hi"], 1)
                    wait(pool, "h_split_hi", b + 3)
                    g.tensor_tensor(h_lo[:, 3:3 + SEQ], h_new[:], h_hi[:, 3:3 + SEQ].bitcast(F32), ALU.subtract).then_inc(S["h_split"], 1)
                pool.drain().then_inc(S["pool_slot"], 1)

            slots(pool, body)

        @block.scalar
        def _(act):
            ac = nc.scalar
            act.wait_ge(S["w_in"], 16 * 13)
            ac.activation(a_neg[:], a_log[:], ACT.Exp).then_inc(S["set_act"], 1)

            def body(s, b, c, has):
                slot_begins(act, s)
                q1 = (b + 1) % 2
                if has(-4) and c < 2:
                    k = 2 * c
                    wait(act, "z_s", (b + 1) * 4 + k - 1)
                    wait(act, "z_mm", (b + 1) * 4 + k + 1)
                    ac.activation(zu[:, 0, :], bank[0][:, 0:DI], ACT.Copy, scale=0.5)
                    ac.activation(zt[:, 0, :], bank[0][:, 0:DI], ACT.Tanh, scale=0.5).then_inc(S["z_act"], 1)
                if has(-4):
                    wait(act, "f_mm", s + 4 + 1)
                    wait(act, "s_xc", b * 4)
                    alone(act, s)
                    ac.activation(cv[:, q1, c, :], bank[1][:], ACT.Identity, scale=0.5, bias=hconv_b[:, c:c + 1]).then_inc(S["f_v"], 1)
                    ac.activation(ct[:, q1, c, :], bank[1][:], ACT.Tanh, scale=0.5, bias=hconv_b[:, c:c + 1]).then_inc(S["f_t"], 1)
                tr = [has(-8), has(2), has(3)]
                if any(tr):
                    wait(act, "t_mm", s - FIRST + 1)
                if tr[0] and c == 0:
                    wait(act, "h_split", b + 2)
                if tr[1]:
                    ac.activation(yt[:, c % 2, :], bank[7][:, P:P + DI], ACT.Copy).then_inc(S["t_y"], 1)
                if tr[0]:
                    ac.activation(h_new[:, c * P:c * P + P], bank[7][:, 0:P], ACT.Identity,
                                  scale=mod[:, 0, 1, bass.ds(b + 2, 1)], bias=mod[:, 0, 0, bass.ds(b + 2, 1)]).then_inc(S["h_staged"], 1)
                if tr[2]:
                    bb = b if c == 3 else b - 1
                    ac.activation(hc[:, (c + 1) % 2, :], bank[7][:, 3 * P:4 * P], ACT.Identity,
                                  scale=mod[:, 0, 4, bass.ds(bb, 1)], bias=mod[:, 0, 3, bass.ds(bb, 1)]).then_inc(S["t_h2"], 1)
                if has(0):
                    wait(act, "s_tr", s + 1)
                    wait(act, "s_smm", s - 1)
                    ac.activation(xb[:, c % 2, :], bank[2][:, 0:3 * P], ACT.Copy).then_inc(S["s_xb"], 1)
                if has(-4) and c < 2:
                    k = 2 * c + 1
                    wait(act, "z_s", (b + 1) * 4 + k - 1)
                    wait(act, "z_mm", (b + 1) * 4 + k + 1)
                    ac.activation(zu[:, 1, :], bank[0][:, 0:DI], ACT.Copy, scale=0.5)
                    ac.activation(zt[:, 1, :], bank[0][:, 0:DI], ACT.Tanh, scale=0.5).then_inc(S["z_act"], 1)
                if has(-4) and c == 2:
                    wait(act, "z_dt", (b + 1) * 4 + 4)
                    ac.activation(dta[:], dtr[:], ACT.Abs).then_inc(S["d_abs"], 1)
                    wait(act, "d_abs", b + 2)
                    ac.activation(dte[:], dta[:], ACT.Exp, scale=-1.0).then_inc(S["d_exp"], 1)
                    wait(act, "d_exp", b + 2)
                    ac.activation(dtl[:], dte[:], ACT.Ln, bias=1.0).then_inc(S["d_ln"], 1)
                    wait(act, "d_dta", b + 2)
                    ac.activation(da[:], dax[:], ACT.Exp).then_inc(S["d_da"], 1)
                if has(1):
                    wait(act, "s_yz", s)
                    wait(act, "s_ss", s - 1)
                    ac.activation(ysq[:], yz[:, (c + 1) % 2, :], ACT.Square, scale=1.0 / 16, accum_out=ss[:, (c + 1) % 2, :]).then_inc(S["s_ss"], 1)
                act.drain().then_inc(S["act_slot"], 1)

            slots(act, body)

        @block.vector
        def _(dve):
            v = nc.vector
            n = [0]

            def step(ins):
                n[0] += 1
                ins.then_inc(S["set_dve"], 1)
                dve.wait_ge(S["set_dve"], n[0])

            step(v.tensor_tensor(res_g[:], rows0[:, :, 1, :], rows0[:, :, 2, :], ALU.mult))
            step(v.tensor_tensor(res_b[:], rows0[:, :, 0, :], rows0[:, :, 2, :], ALU.mult))
            dve.wait_ge(S["set_act"], 1)
            step(v.tensor_scalar(a_neg[:], a_neg[:], -1.0, None, ALU.mult))
            assert n[0] == DVE_SETUP, n[0]
            dve.wait_ge(S["set_pool"], POOL_SETUP)

            def count(n):
                return min(n, NT) if isinstance(n, int) else n

            def y_count(b, c):
                return 3 * b + c - 1 if c else 3 * b

            def body(s, b, c, has):
                slot_begins(dve, s)
                q1 = (b + 1) % 2
                p, pn = c % 2, (c + 1) % 2
                cs = (c - 1) % 4
                qs = b % 2 if c else (b + 1) % 2
                if has(-9):
                    v.bn_stats(st1[:, pn, :], x[:, s + 9, :]).then_inc(S["ln1_stats"], 1)
                wait(dve, "ln1_stats", count(s + 10))
                if has(0):
                    wait(dve, "f_t", b * 4 + 4)
                    wait(dve, "s_ymm", s - 1)
                    v.scalar_tensor_tensor(out=xc[:, p], in0=ct[:, b % 2, :, c * P:c * P + P], scalar=1.0,
                                           in1=cv[:, b % 2, :, c * P:c * P + P], op0=ALU.add, op1=ALU.mult).then_inc(S["s_xc"], 1)
                if has(-9):
                    v.bn_aggr(mv1[:, pn, :], st1[:, pn, :]).then_inc(S["ln1_mv"], 1)

                def z(i):
                    k = 2 * c + i
                    wait(dve, "z_act", (b + 1) * 4 + k + 1)
                    wait(dve, "s_yz", s - 1)
                    v.tensor_tensor(dtr[:, k * NH:k * NH + NH], bank[0][:, DI:DI + NH], dt_b[:], ALU.add).then_inc(S["z_dt"], 1)
                    v.scalar_tensor_tensor(out=zs[:, q1, k, :], in0=zt[:, i, :], scalar=1.0, in1=zu[:, i, :],
                                           op0=ALU.add, op1=ALU.mult).then_inc(S["z_s"], 1)

                if has(-4) and c < 2:
                    z(0)
                if has(-4) and c == 3:
                    wait(dve, "d_tr", b + 2)
                    alone(dve, s)
                    v.tensor_copy(da_t[:, q1, 1:P], bank[4][0:16, 257:384]).then_inc(S["d_tz"], 1)
                    v.tensor_tensor_scan(cum_t[:], bank[4][0:16, 256:384], zero16[:], 1.0, ALU.mult, ALU.add).then_inc(S["d_scan"], 1)
                if has(0):
                    wait(dve, "s_bc", s + 1)
                    v.tensor_tensor_scan(lt[:, p, :], bank[3][:], ident4[:], 0.0, ALU.mult, ALU.add).then_inc(S["s_lt"], 1)
                if has(-9):
                    wait(dve, "t_mm", s - 1 - FIRST + 1)
                    wait(dve, "ln1_rs", s + 10)
                    v.tensor_scalar(xn1[:, pn, :], x[:, s + 9, :], mv1[:, pn, 0:1], rs1[:, pn, :], ALU.subtract, ALU.mult).then_inc(S["ln1_xn"], 1)
                if has(0):
                    wait(dve, "s_lt", s + 1)
                    wait(dve, "s_g", s + 1)
                    wait(dve, "s_ymm", s - 1)
                    v.tensor_tensor(mt[:, p, :].rearrange("p (h i) -> p h i", h=NH), lt[:, p, :].rearrange("p (h i) -> p h i", h=NH),
                                    bank[6][:, DI:DI + P].rearrange("p (o i) -> p o i", o=1).broadcast_to([P, NH, P]),
                                    ALU.mult).then_inc(S["s_mt"], 1)
                if has(-4) and c < 2:
                    z(1)
                if has(-4) and c == 2:
                    wait(dve, "d_ln", b + 2)
                    v.scalar_tensor_tensor(out=dt[:, q1, :], in0=dtr[:], scalar=0.0, in1=dtl[:], op0=ALU.max, op1=ALU.add).then_inc(S["d_dt"], 1)
                if has(-4) and c == 3:
                    wait(dve, "d_tr2", b + 2)
                    alone(dve, s)
                    v.tensor_copy(cum[:, q1, :], bank[4][:, 384:400]).then_inc(S["d_cum"], 1)
                if has(2):
                    wait(dve, "o_mm", s - 1)
                    wait(dve, "s_rr", s - 1)
                    v.scalar_tensor_tensor(out=x[:, s - 2, :], in0=bank[4][:, 0:P], scalar=rr[:, p, :], in1=x[:, s - 2, :],
                                           op0=ALU.mult, op1=ALU.add).then_inc(S["o_x"], 1)
                if has(-4) and c == 2:
                    wait(dve, "d_dt", b + 2)
                    alone(dve, s)
                    v.tensor_tensor(dax[:], dt[:, q1, :], a_neg[:], ALU.mult).then_inc(S["d_dta"], 1)
                if has(1):
                    wait(dve, "s_smm", s)
                    wait(dve, "s_yz", s - 1)
                    wait(dve, "s_xd", s)
                    if cs:
                        alone(dve, s)
                        v.tensor_tensor(hv(y1[:]), hv(bank[5][:, DI:2 * DI]), bc3(cum[:, qs, cs * NH:cs * NH + NH], NH, HD), ALU.mult).then_inc(S["s_y1"], 1)
                    else:
                        v.tensor_tensor(y3[:], bank[5][:, 0:DI], xd[:, pn, :], ALU.add).then_inc(S["s_y3"], 1)
                wait(dve, "o_x", count(s - 1))
                if has(2):
                    alone(dve, s)
                    v.bn_stats(st2[:, p, :], x[:, s - 2, :]).then_inc(S["ln2_stats"], 1)
                if has(1):
                    wait(dve, "s_sd", s)
                    if cs in (1, 2):
                        v.tensor_tensor(state[:], state_d[:], bank[6][:, 0:DI], ALU.add).then_inc(S["s_state"], 1)
                    elif cs == 0:
                        wait(dve, "s_y3", s)
                        v.tensor_copy(state[:], bank[6][:, 0:DI]).then_inc(S["s_state"], 1)
                    if cs:
                        wait(dve, "s_y1", y_count(b, c))
                        v.tensor_tensor(y2[:], y1[:], bank[5][:, 0:DI], ALU.add).then_inc(S["s_y2"], 1)
                wait(dve, "ln2_stats", count(s - 1))
                if has(2):
                    alone(dve, s)
                    v.bn_aggr(mv2[:, p, :], st2[:, p, :]).then_inc(S["ln2_mv"], 1)
                if has(1) and cs:
                    wait(dve, "s_y2", y_count(b, c))
                    v.tensor_tensor(y3[:], y2[:], xd[:, pn, :], ALU.add).then_inc(S["s_y3"], 1)
                if has(-4) and c == 3:
                    wait(dve, "d_mm", b + 2)
                    alone(dve, s)
                    v.tensor_copy(tot[:, q1, :], bank[4][:, 400:416]).then_inc(S["d_tot"], 1)
                if has(3):
                    wait(dve, "r_mm", s - 2)
                    v.tensor_copy(lgc[:, pn, :], bank[4][:, P:P + NE]).then_inc(S["r_lg"], 1)
                wait(dve, "r_lg", count(s - 2))
                if has(1):
                    wait(dve, "s_y3", s)
                    wait(dve, "t_mm", s - 1 - FIRST + 1)
                    if isinstance(s, int):
                        v.tensor_tensor(yz[:, pn, :], y3[:], zs[:, qs, cs, :], ALU.mult).then_inc(S["s_yz"], 1)
                    else:
                        alone(dve, s)
                        v.tensor_tensor(yz[:, pn, :], y3[:], zs[:, qs, cs, :], ALU.mult).then_inc(S["s_yz"], 1)
                if has(3):
                    v.max(mx[:, pn, :], lgc[:, pn, :]).then_inc(S["r_mx"], 1)
                wait(dve, "r_mx", count(s - 2))
                wait(dve, "ln2_rs", count(s - 1))
                wait(dve, "t_mm", s - 1 - FIRST + 1)
                if has(2):
                    v.tensor_scalar(xn2[:, p, :], x[:, s - 2, :], mv2[:, p, 0:1], rs2[:, p, :], ALU.subtract, ALU.mult).then_inc(S["ln2_xn"], 1)
                if has(3):
                    v.max_index(mi[:, pn, :], mx[:, pn, :], lgc[:, pn, :]).then_inc(S["r_mi"], 1)
                if has(3):
                    wait(dve, "r_mi", s - 2)
                    v.tensor_copy(ix[:, s - 3, :], mi[:, pn, 0:2])
                if has(1) and cs == 3:
                    dve.drain().then_inc(S["s_state"], 1)
                dve.drain().then_inc(S["dve_slot"], 1)

            slots(dve, body)

        @block.tensor
        def _(pe):
            t_ = nc.tensor
            pe.wait_ge(S["set_dve"], DVE_SETUP)
            pe.wait_ge(S["set_pool"], POOL_SETUP)

            def split3(dst, l_hi, l_lo, r_hi, r_lo, first, last):
                t_.matmul(dst, l_hi, r_hi, start=first, stop=False)
                t_.matmul(dst, l_lo, r_hi, start=False, stop=False)
                return t_.matmul(dst, l_hi, r_lo, start=False, stop=last)

            def body(s, b, c, has):
                slot_begins(pe, s)
                p, pn = c % 2, (c + 1) % 2
                q, q1 = b % 2, (b + 1) % 2

                def z(i):
                    k = 2 * c + i
                    wait(pe, "z_dt", (b + 1) * 4 + k)
                    split3(bank[0][:, 0:DI + NH], h_hi[:, 3 + k * P:3 + k * P + P], h_lo[:, 3 + k * P:3 + k * P + P],
                           wz_hi[:], wz_lo[:], True, True).then_inc(S["z_mm"], 1)

                if has(-4) and c == 0:
                    wait(pe, "h_split", b + 2)
                if has(-4) and c < 2:
                    z(0)
                if has(-4):
                    wait(pe, "f_t", s + 4)
                    for k in range(NTAP):
                        mm = split3(bank[1][:], wc_hi[:, k, c * P:c * P + P], wc_lo[:, k, c * P:c * P + P],
                                    h_hi[:, k:k + SEQ], h_lo[:, k:k + SEQ], k == 0, k == NTAP - 1)
                    mm.then_inc(S["f_mm"], 1)
                if has(-8) or has(2) or has(3):
                    for name, n in (("h_staged", s + 8), ("t_y", s - 2), ("t_h2", s - 3)):
                        wait(pe, name, min(n, NT) if isinstance(n, int) else n)
                    if has(2):
                        wait(pe, "s_yz", s - 1)
                        for k in range(2):
                            mm = t_.transpose(bank[7][:, P + k * P:2 * P + k * P], yz[:, p, k * P:k * P + P], ident[:])
                    if has(3):
                        wait(pe, "ln2_xn", s - 2)
                        mm = t_.transpose(bank[7][:, 3 * P:4 * P], xn2[:, pn, :], ident[:])
                    if has(-8):
                        wait(pe, "ln1_xn", s + 9)
                        mm = t_.transpose(bank[7][:, 0:P], xn1[:, p, :], ident[:])
                    mm.then_inc(S["t_mm"], 1)
                else:
                    pe.drain().then_inc(S["t_mm"], 1)
                if has(-4) and c == 3:
                    wait(pe, "d_da", b + 2)
                    wait(pe, "r_lg", s - 4 + 1)
                    wait(pe, "o_x", s - 3 + 1)
                    t_.transpose(bank[4][0:16, 256:384], da[:], ident[:]).then_inc(S["d_tr"], 1)
                if has(0):
                    wait(pe, "s_xc", s + 1)
                    wait(pe, "s_xb", s)
                    wait(pe, "s_lt", s)
                    wait(pe, "d_tz", b + 1)
                    for k in range(3):
                        mm = t_.transpose(bank[2][:, k * P:k * P + P], xc[:, p, k, :], ident[:])
                    mm.then_inc(S["s_tr"], 1)
                    for h in range(NH):
                        mm = t_.matmul(bank[3][:, h * P:h * P + P], sel[:, (c * NH + h) * P:(c * NH + h + 1) * P], da_t[:, q, :],
                                       start=True, stop=True)
                    mm.then_inc(S["s_bc"], 1)
                    wait(pe, "s_mt", s)
                    wait(pe, "s_state", s - 1)
                    t_.matmul(bank[6][:, DI:DI + P], xc[:, p, 2, :], xc[:, p, 3, :], start=True, stop=True).then_inc(S["s_g"], 1)
                if has(-4) and c < 2:
                    z(1)
                if has(-4) and c == 3:
                    wait(pe, "d_scan", b + 2)
                    alone(pe, s)
                    t_.transpose(bank[4][:, 384:400], cum_t[:], ident[0:16, 0:16]).then_inc(S["d_tr2"], 1)
                if has(2):
                    wait(pe, "t_y", s - 2 + 1)
                    wait(pe, "r_lg", s - 4 + 1)
                    if has(-4) and c == 3:
                        wait(pe, "d_cum", b + 2)
                    for k in range(2):
                        mm = t_.matmul(bank[4][:, 0:P], yt[:, p, k * P:k * P + P], wo8[:, b - 1 if c < 2 else b, k, :], start=(k == 0), stop=(k == 1))
                    mm.then_inc(S["o_mm"], 1)
                if has(1):
                    cs = (c - 1) % 4
                    wait(pe, "s_mt", s)
                    wait(pe, "s_xdt", s)
                    wait(pe, "s_y3", s - 1)
                    for h in range(NH):
                        mm = t_.matmul(bank[5][:, h * HD:h * HD + HD], mt[:, pn, h * P:h * P + P], xdt[:, pn, h * HD:h * HD + HD],
                                       start=True, stop=True)
                    if cs:
                        wait(pe, "s_state", s - 1)
                        mm = t_.matmul(bank[5][:, DI:2 * DI], xc[:, pn, 3, :], state[:], start=True, stop=True)
                    mm.then_inc(S["s_ymm"], 1)
                    if cs < 3:
                        wait(pe, "s_xdw", s)
                        if has(0):
                            wait(pe, "s_mt", s + 1)
                        t_.matmul(bank[6][:, 0:DI], xb[:, pn, DI:DI + P], xdw[:, pn, :], start=True, stop=True).then_inc(S["s_smm"], 1)
                    else:
                        pe.drain().then_inc(S["s_smm"], 1)
                if has(-4) and c == 3:
                    wait(pe, "d_cum", b + 2)
                    if has(2):
                        wait(pe, "o_x", s - 2 + 1)
                    t_.matmul(bank[4][:, 400:416], sel127[:], cum[:, q1, :], start=True, stop=True).then_inc(S["d_mm"], 1)
                if has(3):
                    wait(pe, "t_h2", s - 3 + 1)
                    wait(pe, "r_lg", s - 3)
                    wait(pe, "o_x", s - 2 + 1 if has(2) else s - 3 + 1)
                    if has(-4) and c == 3:
                        wait(pe, "d_tot", b + 2)
                    t_.matmul(bank[4][:, P:P + NE], hc[:, pn, :], gw[:], start=True, stop=True).then_inc(S["r_mm"], 1)
                pe.drain().then_inc(S["pe_slot"], 1)

            slots(pe, body)


def l0_experts(nc, k, a):
    x, h_all, ones, lg, ix, bank, S = k.x, k.h_all, k.ones, k.lg, k.ix, k.bank, k.S
    wait, alone = k.wait, k.alone
    k.sems(("g_step", "g_cnt", "g_flag", "g_in", "g_sh", "g_exp", "g_comb", "g_hmm", "g_hev", "g_ymm", "g_acc", "g_gated", "g_x"))
    with ExitStack() as ctx:
        sb = lambda name, shape, dt=F32: ctx.enter_context(nc.sbuf_tensor(name, shape, dt))
        m0 = sb("g_m0", [P, NT, NE]); m1 = sb("g_m1", [P, NT, NE])
        mine = sb("g_mine", [P, NE]); keep = sb("g_keep", [P, NE]); any_kept = sb("g_any", [P, 1]); flag = sb("g_flagi", [P, 1], I32)
        peak = sb("g_peak", [P, NT]); ex = sb("g_ex", [P, NT, NE]); total = sb("g_total", [P, NT])
        w1 = sb("g_w1", [P, NE, D]); w2 = sb("g_w2", [P, NE, D]); b1 = sb("g_b1", [P, NE]); b2 = sb("g_b2", [1, NE, D])
        ht = sb("g_ht", [P, 2, SEQ]); acc = sb("g_acc_sb", [P, 2, NC, D]); gated = sb("g_gated_sb", [P, NC, D])
        block = ctx.enter_context(nc.Block())

        def any_expert_kept(e):
            e.wait_ge(S["g_flag"], 1)
            return e.value_load(flag[0:1, 0:1], min_val=0, max_val=1) != 0

        @block.vector
        def _(dve):
            v = nc.vector
            n = [0]

            def step(ins):
                n[0] += 1
                ins.then_inc(S["g_step"], 1)
                dve.wait_ge(S["g_step"], n[0])

            iot = k.iota[:].rearrange("p (o e) -> p o e", o=1).broadcast_to([P, NT, NE])
            step(v.tensor_tensor(m0[:], ix[:, :, 0:1].broadcast_to([P, NT, NE]), iot, ALU.is_equal))
            step(v.tensor_tensor(m1[:], ix[:, :, 1:2].broadcast_to([P, NT, NE]), iot, ALU.is_equal))
            step(v.tensor_tensor(m0[:], m0[:], m1[:], ALU.add))
            step(v.tensor_reduce(mine[:], m0[:].rearrange("p t e -> p e t"), AX.X, ALU.add))
            dve.wait_ge(S["g_cnt"], 1)
            step(v.tensor_scalar(keep[:], bank[0][:, 0:NE], float(CAP), None, ALU.is_le))
            step(v.tensor_reduce(any_kept[:], keep[:], AX.X, ALU.max))
            v.tensor_copy(flag[:], any_kept[:]).then_inc(S["g_flag"], 1)
            with dve.If(any_expert_kept(dve)):
                step(v.tensor_reduce(peak[:], lg[:], AX.X, ALU.max))
                v.tensor_tensor(ex[:], lg[:], bc3(peak[:], NT, NE), ALU.subtract).then_inc(S["g_sh"], 1)
                dve.wait_ge(S["g_exp"], 1)
                step(v.tensor_reduce(total[:], ex[:], AX.X, ALU.add))
                step(v.reciprocal(total[:], total[:]))
                step(v.tensor_tensor(ex[:], ex[:], bc3(total[:], NT, NE), ALU.mult))
                step(v.tensor_tensor(ex[:], ex[:], m0[:], ALU.mult))
                v.tensor_tensor(ex[:], ex[:], keep[:].rearrange("p (o e) -> p o e", o=1).broadcast_to([P, NT, NE]), ALU.mult).then_inc(S["g_comb"], 1)
                dve.wait_ge(S["g_comb"], 1)
                def sequence(b):
                    for e in range(NE):
                        wait(dve, "g_ymm", b * NE + e + 1)
                        if e == 0:
                            wait(dve, "g_gated", b)
                        wait(dve, "g_acc", (b * NE + e) * NC)
                        for c in range(NC):
                            w = ex[:, b * NC + c, e:e + 1]
                            y = bank[4 + e % 2][:, c * P:c * P + P]
                            if e == 0:
                                v.tensor_scalar(acc[:, 1, c, :], y, w, None, ALU.mult).then_inc(S["g_acc"], 1)
                            else:
                                v.scalar_tensor_tensor(out=acc[:, (e + 1) % 2, c, :], in0=y, scalar=w, in1=acc[:, e % 2, c, :],
                                                       op0=ALU.mult, op1=ALU.add).then_inc(S["g_acc"], 1)

                sequence(0)
                with dve.Fori(1, NB) as b:
                    sequence(b)

        @block.sync
        def _(sp):
            with sp.If(any_expert_kept(sp)):
                for dst, key in ((w1, "g_w1"), (w2, "g_w2"), (b1, "g_b1"), (b2, "g_b2")):
                    sp.dma_start(dst[:], a[key]).then_inc(S["g_in"], 16)
                sp.wait_ge(S["g_in"], 64)

        @block.gpsimd
        def _(pool):
            g = nc.gpsimd
            with pool.If(any_expert_kept(pool)):
                def sequence(b):
                    wait(pool, "g_acc", (b + 1) * NE * NC)
                    wait(pool, "g_x", b)
                    alone(pool, b)
                    for c in range(NC):
                        ins = g.tensor_tensor(gated[:, c, :], acc[:, 0, c, :], k.gate_rows[:, 0, b, :], ALU.mult)
                    ins.then_inc(S["g_gated"], 1)
                    wait(pool, "g_gated", b + 1)
                    alone(pool, b)
                    g.tensor_tensor(x[:, bass.ds(b * NC, NC), :], x[:, bass.ds(b * NC, NC), :], gated[:], ALU.add).then_inc(S["g_x"], 1)

                sequence(0)
                with pool.Fori(1, NB) as b:
                    sequence(b)

        @block.scalar
        def _(act):
            ac = nc.scalar
            with act.If(any_expert_kept(act)):
                act.wait_ge(S["g_sh"], 1)
                ac.activation(ex[:], ex[:], ACT.Exp).then_inc(S["g_exp"], 1)
                act.wait_ge(S["g_in"], 64)
                def sequence(b):
                    for e in range(NE):
                        wait(act, "g_hmm", b * NE + e + 1)
                        alone(act, b)
                        ac.activation(ht[:, e % 2, :], bank[e % 2][:], ACT.Relu, bias=b1[:, e:e + 1]).then_inc(S["g_hev"], 1)

                sequence(0)
                with act.Fori(1, NB) as b:
                    sequence(b)

        @block.tensor
        def _(pe):
            t_ = nc.tensor
            pe.wait_ge(S["g_step"], 4)
            t_.matmul(bank[0][:, 0:NE], ones[:], mine[:], start=True, stop=True).then_inc(S["g_cnt"], 1)
            with pe.If(any_expert_kept(pe)):
                pe.wait_ge(S["g_in"], 64)

                def hidden(b, e):
                    wait(pe, "g_hev", b * NE + e)
                    t_.matmul(bank[e % 2][:], w1[:, e, :], h_all[:, b, :], start=True, stop=True).then_inc(S["g_hmm"], 1)

                def sequence(b):
                    hidden(b, 0)
                    for e in range(NE):
                        wait(pe, "g_hev", b * NE + e + 1)
                        wait(pe, "g_acc", (b * NE + e) * NC)
                        for c in range(NC):
                            y = bank[4 + e % 2][:, c * P:c * P + P]
                            t_.matmul(y, ht[:, e % 2, c * P:c * P + P], w2[:, e, :], start=True, stop=False)
                            mm = t_.matmul(y, ones[0:1, :], b2[:, e, :], start=False, stop=True)
                        mm.then_inc(S["g_ymm"], 1)
                        if e + 1 < NE:
                            hidden(b, e + 1)

                sequence(0)
                with pe.Fori(1, NB) as b:
                    sequence(b)


def attention(nc, k, a):
    x, h_all, ident, mod, lg, bank, S = k.x, k.h_all, k.ident, k.mod, k.lg, k.bank, k.S
    wait, alone = k.wait, k.alone
    k.sems(("a_set", "a_stats", "a_mv", "a_ve", "a_rs", "a_xn", "a_t", "a_h",
            "q_mm", "k_mm", "v_mm", "q_ev", "k_ev", "v_ev", "wo_g", "bo_x",
            "sc_mm", "sc_max", "sc_exp", "p_t", "p_ev", "p_rinv", "ot_mm", "ot_ev", "op_mm", "op_x",
            "b_stats", "b_mv", "b_ve", "b_rs", "b_xn", "b_t", "b_h", "b_keep", "b_lg_mm", "b_lg"))
    with ExitStack() as ctx:
        sb = lambda name, shape, dt=F32: ctx.enter_context(nc.sbuf_tensor(name, shape, dt))
        st_a = sb("st_a", [P, NC, 6]); mv_a = sb("mv_a", [P, NC, 2]); ve_a = sb("ve_a", [P, NC]); rs_a = sb("rs_a", [P, NC])
        st_b = sb("st_b", [P, NC, 6]); mv_b = sb("mv_b", [P, NC, 2]); ve_b = sb("ve_b", [P, NC]); rs_b = sb("rs_b", [P, NC])
        xn_a = sb("xn_a", [P, NC, D]); xn_b = sb("xn_b", [P, NC, D])
        h3 = sb("h3", [P, SEQ]); h4 = sb("h4", [P, SEQ])
        bq = sb("bq", [P, 1])
        wog = sb("wog", [P, D])
        bog = sb("bog", [P, NB, D])
        qT = sb("qT", [P, SEQ]); kT = sb("kT", [P, SEQ]); vv = sb("vv", [P, NC, D])
        nmx = sb("nmx", [P, NC]); sm = sb("sm", [P, NC]); rinv = sb("rinv", [P, NC])
        pr = sb("pr", [P, NC, SEQ]); pt = sb("pt", [P, NC, SEQ])
        oT = sb("oT", [P, SEQ])
        wq, wk, wv, wo = (k.attn_w[:, i, :] for i in range(4))
        block = ctx.enter_context(nc.Block())

        def run(e, body):
            body(-1, True, False, False)
            body(0, True, True, False)
            body(1, True, True, True)
            with e.Fori(2, NB - 1) as s:
                body(s, True, True, True)
            body(NB - 1, False, True, True)
            body(NB, False, False, True)

        def rows(s):
            return bass.ds(s * NC, NC)

        @block.gpsimd
        def _(pool):
            g = nc.gpsimd
            for b in range(NB):
                g.tensor_tensor(bog[:, b, :], k.bo[:], k.gate_rows[:, 1, b, :], ALU.mult)
            g.tensor_scalar(bq[:], k.attn_b[:, 0:1], 0.125, None, ALU.mult).then_inc(S["a_set"], 1)
            pool.wait_ge(S["a_set"], 1)

            def body(s, A, B, C):
                if A:
                    wait(pool, "a_mv", NC * (s + 2))
                    g.tensor_tensor(ve_a[:], mv_a[:].rearrange("p c t -> p (c t)")[:, 1::2], k.eps[:], ALU.add).then_inc(S["a_ve"], 1)
                    wait(pool, "a_ve", s + 2)
                    g.tensor_tensor(rs_a[:], ve_a[:], k.half_neg[:], ALU.pow).then_inc(S["a_rs"], 1)
                if B:
                    wait(pool, "a_xn", NC * (s + 1))
                    alone(pool, s)
                    for c in range(NC):
                        ins = g.tensor_tensor(x[:, s * NC + c, :], x[:, s * NC + c, :], bog[:, s, :], ALU.add)
                    ins.then_inc(S["bo_x"], 1)
                    wait(pool, "op_mm", s)
                    alone(pool, s)
                    g.tensor_tensor(wog[:], wo, k.gate_rows[:, 1, s, :], ALU.mult).then_inc(S["wo_g"], 1)
                if C:
                    wait(pool, "b_mv", NC * s)
                    g.tensor_tensor(ve_b[:], mv_b[:].rearrange("p c t -> p (c t)")[:, 1::2], k.eps[:], ALU.add).then_inc(S["b_ve"], 1)
                    wait(pool, "b_ve", s)
                    g.tensor_tensor(rs_b[:], ve_b[:], k.half_neg[:], ALU.pow).then_inc(S["b_rs"], 1)
                    wait(pool, "b_h", s)
                    alone(pool, s)
                    g.tensor_copy(h_all[:, s - 1, :], h4[:]).then_inc(S["b_keep"], 1)

            run(pool, body)

        @block.scalar
        def _(act):
            ac = nc.scalar
            act.wait_ge(S["a_set"], 1)

            def body(s, A, B, C):
                if C:
                    wait(act, "ot_mm", s)
                    ac.activation(oT[:], bank[0][:], ACT.Copy).then_inc(S["ot_ev"], 1)
                if B:
                    wait(act, "q_mm", s + 1)
                    ac.activation(qT[:], bank[1][:], ACT.Identity, scale=0.125, bias=bq[:]).then_inc(S["q_ev"], 1)
                    wait(act, "k_mm", s + 1)
                    ac.activation(kT[:], bank[2][:], ACT.Identity, bias=k.attn_b[:, 1:2]).then_inc(S["k_ev"], 1)
                for c in range(NC):
                    if B:
                        wait(act, "sc_max", NC * s + c + 1)
                        ac.activation(pr[:, c, :], bank[5 + c % 2][:], ACT.Exp, bias=nmx[:, c:c + 1], accum_out=sm[:, c:c + 1]).then_inc(S["sc_exp"], 1)
                    if A and c == 1:
                        wait(act, "a_t", s + 2)
                        alone(act, s)
                        ac.activation(h3[:], bank[0][:], ACT.Identity, scale=mod[:, 1, 1, bass.ds(s + 1, 1)],
                                      bias=mod[:, 1, 0, bass.ds(s + 1, 1)]).then_inc(S["a_h"], 1)
                if C:
                    wait(act, "b_t", s)
                    wait(act, "b_keep", s - 1)
                    alone(act, s)
                    ac.activation(h4[:], bank[1][:], ACT.Identity, scale=mod[:, 1, 4, bass.ds(s - 1, 1)],
                                  bias=mod[:, 1, 3, bass.ds(s - 1, 1)]).then_inc(S["b_h"], 1)

            run(act, body)

        @block.vector
        def _(dve):
            v = nc.vector

            def body(s, A, B, C):
                if A:
                    for c in range(NC):
                        v.bn_stats(st_a[:, c, :], x[:, (s + 1) * NC + c, :]).then_inc(S["a_stats"], 1)
                    wait(dve, "a_rs", s + 1)
                    wait(dve, "a_stats", NC * (s + 2))
                    alone(dve, s)
                    for c in range(NC):
                        v.bn_aggr(mv_a[:, c, :], st_a[:, c, :]).then_inc(S["a_mv"], 1)
                if B:
                    wait(dve, "v_mm", s + 1)
                    v.tensor_tensor(vv[:], bank[3][:].rearrange("p (c d) -> p c d", c=NC),
                                    k.bv[:].rearrange("p (o d) -> p o d", o=1).broadcast_to([P, NC, D]), ALU.add).then_inc(S["v_ev"], 1)
                if A:
                    wait(dve, "a_rs", s + 2)
                    wait(dve, "a_t", s + 1)
                    for c in range(NC):
                        v.tensor_scalar(xn_a[:, c, :], x[:, (s + 1) * NC + c, :], mv_a[:, c, 0:1], rs_a[:, c:c + 1],
                                        ALU.subtract, ALU.mult).then_inc(S["a_xn"], 1)
                if C:
                    wait(dve, "op_mm", s)
                    wait(dve, "bo_x", s)
                    wait(dve, "p_rinv", s)
                    for c in range(NC):
                        v.scalar_tensor_tensor(out=x[:, (s - 1) * NC + c, :], in0=bank[4][:, c * P:c * P + P], scalar=rinv[:, c:c + 1],
                                               in1=x[:, (s - 1) * NC + c, :], op0=ALU.mult, op1=ALU.add).then_inc(S["op_x"], 1)
                    wait(dve, "op_x", NC * s)
                    alone(dve, s)
                    for c in range(NC):
                        v.bn_stats(st_b[:, c, :], x[:, (s - 1) * NC + c, :]).then_inc(S["b_stats"], 1)
                    wait(dve, "b_stats", NC * s)
                    wait(dve, "b_xn", NC * (s - 1))
                    alone(dve, s)
                    for c in range(NC):
                        v.bn_aggr(mv_b[:, c, :], st_b[:, c, :]).then_inc(S["b_mv"], 1)
                for c in range(NC):
                    if B:
                        wait(dve, "sc_mm", NC * s + c + 1)
                        alone(dve, s)
                        v.tensor_reduce(nmx[:, c:c + 1], bank[5 + c % 2][:], AX.X, ALU.max, negate=True).then_inc(S["sc_max"], 1)
                    if C and c == 1:
                        wait(dve, "b_rs", s)
                        wait(dve, "b_t", s - 1)
                        for c2 in range(NC):
                            v.tensor_scalar(xn_b[:, c2, :], x[:, (s - 1) * NC + c2, :], mv_b[:, c2, 0:1], rs_b[:, c2:c2 + 1],
                                            ALU.subtract, ALU.mult).then_inc(S["b_xn"], 1)
                if B:
                    for c in range(NC):
                        wait(dve, "p_t", NC * s + c + 1)
                        v.tensor_copy(pt[:, :, c * P:c * P + P], bank[7 if c % 2 == 0 else 3][:].rearrange("p (k q) -> p k q", k=NC)).then_inc(S["p_ev"], 1)
                    wait(dve, "op_x", NC * s)
                    alone(dve, s)
                    v.reciprocal(rinv[:], sm[:]).then_inc(S["p_rinv"], 1)
                if C:
                    wait(dve, "b_lg_mm", s)
                    alone(dve, s)
                    v.tensor_tensor(lg[:, rows(s - 1), :], bank[2][:, 0:NC * NE].rearrange("p (c e) -> p c e", c=NC),
                                    k.br[:].rearrange("p (o e) -> p o e", o=1).broadcast_to([P, NC, NE]), ALU.add).then_inc(S["b_lg"], 1)

            run(dve, body)

        @block.tensor
        def _(pe):
            t_ = nc.tensor

            def body(s, A, B, C):
                if C:
                    wait(pe, "p_ev", NC * s)
                    wait(pe, "a_h", s + 1 if A or B else NB)
                    for i in range(NC):
                        mm = t_.matmul(bank[0][:], vv[:, i, :], pt[:, i, :], start=(i == 0), stop=(i == NC - 1))
                    mm.then_inc(S["ot_mm"], 1)
                if B:
                    wait(pe, "a_h", s + 1)
                    wait(pe, "b_h", s - 1)
                    t_.matmul(bank[1][:], wq, h3[:], start=True, stop=True).then_inc(S["q_mm"], 1)
                    wait(pe, "b_lg", s - 1)
                    t_.matmul(bank[2][:], wk, h3[:], start=True, stop=True).then_inc(S["k_mm"], 1)
                    wait(pe, "p_ev", NC * s)
                    for c in range(NC):
                        mm = t_.matmul(bank[3][:, c * P:c * P + P], h3[:, c * P:c * P + P], wv, start=True, stop=True)
                    mm.then_inc(S["v_mm"], 1)
                if C:
                    wait(pe, "ot_ev", s)
                    wait(pe, "wo_g", s)
                    wait(pe, "op_x", NC * (s - 1))
                    for c in range(NC):
                        mm = t_.matmul(bank[4][:, c * P:c * P + P], oT[:, c * P:c * P + P], wog[:], start=True, stop=True)
                    mm.then_inc(S["op_mm"], 1)
                if B:
                    wait(pe, "q_ev", s + 1)
                    wait(pe, "k_ev", s + 1)
                    for c in range(NC):
                        wait(pe, "sc_exp", NC * s + c - 1)
                        t_.matmul(bank[5 + c % 2][:], qT[:, c * P:c * P + P], kT[:], start=True, stop=True).then_inc(S["sc_mm"], 1)
                if A:
                    wait(pe, "ot_ev", s)
                    wait(pe, "a_h", s + 1)
                    wait(pe, "a_xn", NC * (s + 2))
                    for c in range(NC):
                        mm = t_.transpose(bank[0][:, c * P:c * P + P], xn_a[:, c, :], ident[:])
                    mm.then_inc(S["a_t"], 1)
                if B:
                    for c in range(NC):
                        wait(pe, "sc_exp", NC * s + c + 1)
                        wait(pe, "p_ev", NC * s + c - 1)
                        if c == 1:
                            wait(pe, "v_ev", s + 1)
                        for i in range(NC):
                            mm = t_.transpose(bank[7 if c % 2 == 0 else 3][:, i * P:i * P + P], pr[:, c, i * P:i * P + P], ident[:])
                        mm.then_inc(S["p_t"], 1)
                if C:
                    wait(pe, "b_xn", NC * s)
                    wait(pe, "q_ev", s + 1 if B else NB)
                    for c in range(NC):
                        mm = t_.transpose(bank[1][:, c * P:c * P + P], xn_b[:, c, :], ident[:])
                    mm.then_inc(S["b_t"], 1)
                    wait(pe, "b_h", s)
                    wait(pe, "k_ev", s + 1 if B else NB)
                    for c in range(NC):
                        mm = t_.matmul(bank[2][:, c * NE:c * NE + NE], h4[:, c * P:c * P + P], k.wr[:], start=True, stop=True)
                    mm.then_inc(S["b_lg_mm"], 1)

            run(pe, body)


def l1_experts(nc, k, a, out):
    x, h_all, ident, lg, bank, S = k.x, k.h_all, k.ident, k.lg, k.bank, k.S
    wait, alone = k.wait, k.alone
    k.sems(("e_in", "e_set", "e_max", "e_w", "e_exp", "e_wready", "h_mm", "h_ev", "y_mm", "y_acc", "i_copy", "i_wt", "i_wts", "i_mm", "i_ev",
            "f_stats", "f_mv", "f_ve", "f_rs", "f_n", "f_x", "f_x2", "e_out"))
    with ExitStack() as ctx:
        sb = lambda name, shape, dt=F32: ctx.enter_context(nc.sbuf_tensor(name, shape, dt))
        w1 = sb("w1", [P, NE, FF]); w2 = sb("w2", [P, NE, NG, D])
        b1 = sb("b1", [P, NE, NG]); b2 = sb("b2", [NC * NE, NC * D])
        gamma = sb("gamma", [P, D]); beta = sb("beta", [P, D])
        gg = sb("gg", [P, NB, D]); gb = sb("gb", [P, NB, D])
        top = sb("top", [P, NT, NE]); top_i = sb("top_i", [P, NT, NE], U32); topf = sb("topf", [P, NT, 2])
        ew = sb("ew", [P, NT]); wa = sb("wa", [P, NT]); m0 = sb("m0", [P, NT, NE]); m1 = sb("m1", [P, NT, NE])
        wgt = sb("wgt", [P, NT, NE])
        hc = sb("hc4", [P, SEQ]); wc = sb("wc", [P, NC * NE]); wt = sb("wt", [NC * NE, P])
        ht = sb("ht", [P, 2, NG, SEQ])
        acc = sb("acc", [P, 2, NC, D])
        st = sb("st_f", [P, NC, 6]); mv = sb("mv_f", [P, NC, 2]); ve = sb("ve_f", [P, NC]); rs = sb("rs_f", [P, NC])
        nn = sb("nn", [P, NC, D]); ng = sb("ng", [P, NC, D])
        block = ctx.enter_context(nc.Block())
        IN = 6

        @block.sync
        def _(sp):
            for dst, key in ((w1, "w1"), (b1, "b1"), (w2, "w2"), (b2, "b2"), (gamma, "gamma"), (beta, "beta")):
                sp.dma_start(dst[:], a[key]).then_inc(S["e_in"], 16)
            ov = out.rearrange("b (c p) d -> p (b c) d", p=P)
            with sp.Fori(0, NB) as b:
                wait(sp, "f_x2", b + 1)
                sp.dma_start(ov[:, bass.ds(b * NC, NC), :], x[:, bass.ds(b * NC, NC), :]).then_inc(S["e_out"], 16)
            sp.wait_ge(S["e_out"], 16 * NB)

        @block.gpsimd
        def _(pool):
            g = nc.gpsimd
            pool.wait_ge(S["e_in"], 16 * IN)
            for b in range(NB):
                g.tensor_tensor(gg[:, b, :], gamma[:], k.gate_rows[:, 2, b, :], ALU.mult)
                g.tensor_tensor(gb[:, b, :], beta[:], k.gate_rows[:, 2, b, :], ALU.mult)
            g.drain().then_inc(S["e_set"], 1)
            pool.wait_ge(S["e_set"], 1)
            pool.wait_ge(S["e_wready"], 1)

            def copies(b, b_val):
                wait(pool, "i_mm", b_val)
                alone(pool, b_val)
                g.tensor_copy(hc[:], h_all[:, b, :])
                g.tensor_copy(wc[:].rearrange("p (c e) -> p c e", c=NC), wgt[:, bass.ds(b * NC, NC), :]).then_inc(S["i_copy"], 1)

            copies(0, 0)

            def body(b, last):
                if not last:
                    copies(b + 1, b + 1)
                wait(pool, "f_mv", NC * (b + 1))
                g.tensor_tensor(ve[:], mv[:].rearrange("p c t -> p (c t)")[:, 1::2], k.eps[:], ALU.add).then_inc(S["f_ve"], 1)
                wait(pool, "f_ve", b + 1)
                g.tensor_tensor(rs[:], ve[:], k.half_neg[:], ALU.pow).then_inc(S["f_rs"], 1)
                wait(pool, "f_n", b + 1)
                alone(pool, b)
                for c in range(NC):
                    g.tensor_tensor(ng[:, c, :], nn[:, c, :], gg[:, b, :], ALU.mult)
                    ins = g.tensor_tensor(x[:, b * NC + c, :], x[:, b * NC + c, :], gb[:, b, :], ALU.add)
                ins.then_inc(S["f_x"], 1)
                wait(pool, "f_x", b + 1)
                alone(pool, b)
                g.tensor_tensor(x[:, bass.ds(b * NC, NC), :], x[:, bass.ds(b * NC, NC), :], ng[:], ALU.add).then_inc(S["f_x2"], 1)

            body(0, False)
            with pool.Fori(1, NB - 1) as b:
                body(b, False)
            body(NB - 1, True)

        @block.scalar
        def _(act):
            ac = nc.scalar
            act.wait_ge(S["e_w"], 1)
            ac.activation(ew[:], ew[:], ACT.Exp).then_inc(S["e_exp"], 1)
            act.wait_ge(S["e_in"], 16 * IN)

            def body(b, first):
                for e in range(NE):
                    for i in range(NG):
                        wait(act, "h_mm", (b * NE + e) * NG + i + 1)
                        if i == 0:
                            wait(act, "y_mm", b * NE + e - 1)
                        alone(act, b) if not first and i == 0 else None
                        ac.activation(ht[:, e % 2, i, :], bank[i][:], ACT.Relu, bias=b1[:, e, i:i + 1]).then_inc(S["h_ev"], 1)

            body(0, True)
            with act.Fori(1, NB) as b:
                body(b, False)

        @block.vector
        def _(dve):
            v = nc.vector
            n = [0]

            def step(ins):
                n[0] += 1
                ins.then_inc(S["e_max"], 1)
                dve.wait_ge(S["e_max"], n[0])

            for t in range(NT):
                v.max(top[:, t, :], lg[:, t, :]).then_inc(S["e_max"], 1)
            dve.wait_ge(S["e_max"], NT)
            n[0] = NT
            for t in range(NT):
                v.max_index(top_i[:, t, :], top[:, t, :], lg[:, t, :]).then_inc(S["e_max"], 1)
            n[0] = 2 * NT
            dve.wait_ge(S["e_max"], n[0])
            v.tensor_tensor(ew[:].rearrange("p (t o) -> p t o", o=1), top[:, :, 1:2], top[:, :, 0:1], ALU.subtract).then_inc(S["e_w"], 1)
            step(v.tensor_copy(topf[:], top_i[:, :, 0:2]))
            iot = k.iota[:].rearrange("p (o e) -> p o e", o=1).broadcast_to([P, NT, NE])
            step(v.tensor_tensor(m0[:], topf[:, :, 0:1].broadcast_to([P, NT, NE]), iot, ALU.is_equal))
            step(v.tensor_tensor(m1[:], topf[:, :, 1:2].broadcast_to([P, NT, NE]), iot, ALU.is_equal))
            dve.wait_ge(S["e_exp"], 1)
            step(v.tensor_scalar(wa[:], ew[:], 1.0, None, ALU.add))
            step(v.reciprocal(wa[:], wa[:]))
            step(v.tensor_tensor(ew[:], ew[:], wa[:], ALU.mult))
            step(v.tensor_tensor(m0[:], m0[:], bc3(wa[:], NT, NE), ALU.mult))
            step(v.tensor_tensor(m1[:], m1[:], bc3(ew[:], NT, NE), ALU.mult))
            v.tensor_tensor(wgt[:], m0[:], m1[:], ALU.add).then_inc(S["e_wready"], 1)
            dve.wait_ge(S["e_wready"], 1)

            def body(b, first):
                wait(dve, "i_wt", b + 1)
                alone(dve, b)
                v.tensor_copy(wt[:], bank[6][0:NC * NE, 0:P]).then_inc(S["i_wts"], 1)
                wait(dve, "i_mm", b + 1)
                v.tensor_copy(acc[:, 0], bank[7][:].rearrange("p (c d) -> p c d", c=NC)).then_inc(S["i_ev"], 1)
                wait(dve, "i_ev", b + 1)
                for e in range(NE):
                    wait(dve, "y_mm", b * NE + e + 1)
                    wait(dve, "y_acc", (b * NE + e) * NC)
                    for c in range(NC):
                        v.scalar_tensor_tensor(out=acc[:, (e + 1) % 2, c, :], in0=bank[4 + e % 2][:, c * P:c * P + P],
                                               scalar=wgt[:, b * NC + c, e:e + 1], in1=acc[:, e % 2, c, :],
                                               op0=ALU.mult, op1=ALU.add).then_inc(S["y_acc"], 1)
                wait(dve, "y_acc", (b + 1) * NE * NC)
                alone(dve, b)
                for c in range(NC):
                    v.bn_stats(st[:, c, :], acc[:, 0, c, :]).then_inc(S["f_stats"], 1)
                wait(dve, "f_stats", NC * (b + 1))
                alone(dve, b)
                for c in range(NC):
                    v.bn_aggr(mv[:, c, :], st[:, c, :]).then_inc(S["f_mv"], 1)
                wait(dve, "f_rs", b + 1)
                for c in range(NC):
                    ins = v.tensor_scalar(nn[:, c, :], acc[:, 0, c, :], mv[:, c, 0:1], rs[:, c:c + 1], ALU.subtract, ALU.mult)
                ins.then_inc(S["f_n"], 1)
                wait(dve, "f_n", b + 1)

            body(0, True)
            with dve.Fori(1, NB) as b:
                body(b, False)

        @block.tensor
        def _(pe):
            t_ = nc.tensor
            pe.wait_ge(S["e_in"], 16 * IN)

            def hidden(b, e, b_int):
                for i in range(NG):
                    wait(pe, "h_ev", (b * NE + e - 1) * NG + i + 1)
                    t_.matmul(bank[i][:], w1[:, e, i * P:i * P + P], h_all[:, b, :], start=True, stop=True).then_inc(S["h_mm"], 1)

            def body(b, first):
                hidden(b, 0, b)
                wait(pe, "i_copy", b + 1)
                t_.transpose(bank[6][0:NC * NE, 0:P], wc[:], ident[:]).then_inc(S["i_wt"], 1)
                wait(pe, "i_wts", b + 1)
                wait(pe, "i_ev", b)
                for c in range(NC):
                    t_.matmul(bank[7][:, c * P:c * P + P], wt[:], b2[:, c * D:c * D + D], start=True, stop=False)
                    mm = t_.matmul(bank[7][:, c * P:c * P + P], hc[:, c * P:c * P + P], ident[:], start=False, stop=True)
                mm.then_inc(S["i_mm"], 1)
                for e in range(NE):
                    if e + 1 < NE:
                        hidden(b, e + 1, b)
                    wait(pe, "h_ev", (b * NE + e + 1) * NG)
                    if not (first and e < 2):
                        wait(pe, "y_acc", (b * NE + e - 1) * NC)
                    for c in range(NC):
                        for i in range(NG):
                            mm = t_.matmul(bank[4 + e % 2][:, c * P:c * P + P], ht[:, e % 2, i, c * P:c * P + P], w2[:, e, i, :],
                                           start=(i == 0), stop=(i == NG - 1))
                    mm.then_inc(S["y_mm"], 1)

            body(0, True)
            with pe.Fori(1, NB) as b:
                body(b, False)


def build_program(nc, a, out):
    with ExitStack() as ctx:
        k = Chip(nc, a, ctx)
        conditioning(nc, k, a)
        mixer(nc, k, a)
        l0_experts(nc, k, a)
        attention(nc, k, a)
        l1_experts(nc, k, a, out)


def _layouts(i):
    import numpy as np
    f = lambda v: np.ascontiguousarray(v)
    rep = lambda v: np.ascontiguousarray(np.broadcast_to(v, (P,) + v.shape))
    w = i["L0_attn_in_proj_w"]
    eye = np.eye(P, dtype=np.float32)
    sel = np.zeros((16, 16, P), np.float32)
    for k in range(16):
        sel[k, k] = 1
    sel127 = np.zeros((P, P), np.float32)
    sel127[P - 1] = 1
    b2 = np.zeros((NC, NE, NC, D), np.float32)
    for c in range(NC):
        b2[c, :, c] = i["L1_ffn_b2"]
    return {
        "x": f(i["L0_attn_x"]),
        "cT": f(np.concatenate([i["L0_c"].T, i["L1_c"].T], 1)),
        "wmod": f(np.stack([i["L0_wmod"], i["L1_wmod"]], 1)),
        "w_xbc": f(w[DI:DI + 512].T),
        "w_zdt": f(np.concatenate([w[:DI], w[DI + 512:]]).T),
        "conv_w": rep(i["L0_attn_conv_w"].T),
        "conv_b": f(i["L0_attn_conv_b"].reshape(4, P).T),
        "dt_b": rep(i["L0_attn_dt_bias"]),
        "a_log": rep(np.tile(i["L0_attn_A_log"], NC)),
        "d_bc": rep(np.repeat(i["L0_attn_D"], HD)),
        "norm_w": f(i["L0_attn_norm_w"].reshape(2, P).T),
        "w_out": f(i["L0_attn_out_proj_w"].T.reshape(2, P, D).transpose(1, 0, 2)),
        "gate_w": f(i["L0_ffn_gate_w"].T),
        "ident": eye, "ident4": f(np.tile(eye, (1, NC))), "sel": f(sel.reshape(16, 16 * P)), "sel127": sel127,
        "iota": rep(np.arange(NE, dtype=np.float32)),
        "g_w1": f(i["L0_ffn_W1"].transpose(1, 0, 2)), "g_w2": f(i["L0_ffn_W2"].transpose(1, 0, 2)),
        "g_b1": f(i["L0_ffn_b1"].T), "g_b2": f(i["L0_ffn_b2"][None]),
        "attn_w": f(np.stack([i[f"L1_attn_W{n}"].T for n in "qkvo"], 1)),
        "attn_b": f(np.stack([i["L1_attn_bq"], i["L1_attn_bk"]], 1)),
        "bv": rep(i["L1_attn_bv"]), "bo": rep(i["L1_attn_bo"]),
        "wr": f(i["L1_ffn_Wr"].T), "br": rep(i["L1_ffn_br"]),
        "w1": f(i["L1_ffn_W1"].transpose(2, 0, 1)),
        "b1": f(i["L1_ffn_b1"].reshape(NE, NG, P).transpose(2, 0, 1)),
        "w2": f(i["L1_ffn_W2"].reshape(NE, D, NG, P).transpose(3, 0, 2, 1)),
        "b2": f(b2.reshape(NC * NE, NC * D)),
        "gamma": rep(i["L1_ffn_gamma"]), "beta": rep(i["L1_ffn_beta"]),
    }


def kernel(**inputs):
    import numpy as _np
    import concourse.bacc as _bacc
    from concourse import mybir as _mybir
    from concourse.bass_utils import run_bass_kernel_spmd as _run

    nc = _bacc.Bacc("TRN2", target_bir_lowering=False, num_devices=1)
    arrays, args = {}, {}
    for name, v in _layouts({n: _np.asarray(v) for n, v in inputs.items()}).items():
        arrays["in_" + name] = v
        args[name] = nc.dram_tensor("in_" + name, v.shape, _mybir.dt.from_np(v.dtype), kind="ExternalInput").ap()
    out = nc.dram_tensor("out_x", (NB, SEQ, D), F32, kind="ExternalOutput").ap()
    build_program(nc, args, out)
    r = _run(nc, [arrays], core_ids=[0])
    return r.results[0]["out_x"]
```

```python
from contextlib import ExitStack

import concourse.bass as bass
from concourse import mybir

P = 128
F32 = mybir.dt.float32
F32R = mybir.dt.float32r
I32 = mybir.dt.int32
U32 = mybir.dt.uint32
ALU = mybir.AluOpType
ACT = mybir.ActivationFunctionType
AX = mybir.AxisListType

NB = 8
SEQ = 512
NC = SEQ // P
NT = NB * NC
D = 128
DI = 256
NH = 4
HD = DI // NH
NTAP = 4
NE = 8
FF = 512
NG = FF // P
EPS = 1e-5
CAP = int(1.25 * NB * SEQ / NE)
NTOK = NB * SEQ
REGION = NTOK + P
TILES = 2 * NTOK // P + NE
ROW = D + 4


class Chip:

    def __init__(self, nc, a, ctx):
        self.nc, self.a, self.ctx = nc, a, ctx
        self.bank = [ctx.enter_context(nc.psum_tensor(f"bank{i}", [P, 512], F32)) for i in range(8)]
        self.S = {}
        self.base = {}
        self.retired = []
        sb = lambda name, shape, dt=F32: ctx.enter_context(nc.sbuf_tensor(name, shape, dt))
        self.x = sb("x", [P, NT, D])
        self.h_all = sb("h_all", [P, NB, SEQ])
        self.ident = sb("ident", [P, P])
        self.ones = sb("ones", [P, P])
        self.half_neg = sb("half_neg", [P, NC])
        self.eps = sb("eps", [P, NC])
        self.mod = sb("mod", [P, 2, 6, NB])
        self.rows0 = sb("rows0", [P, NB, 3, D])
        self.moe_rows = sb("moe_rows", [P, NB, 2, D])
        self.gate_rows = sb("gate_rows", [P, 3, NB, D])
        self.lg = sb("lg", [P, NT, NE])
        self.ix = sb("ix", [P, NT, 2])
        self.iota = sb("iota", [P, NE])
        self.filled = sb("filled", [P, NE])
        self.top_w = sb("top_w", [P, 2, NT])
        self.queue = nc.dram_tensor("queue", (NE * REGION + NE * P, ROW), F32).ap()
        self.results = nc.dram_tensor("results", (2 * NTOK + 2 * NE * P, D), F32).ap()
        self.attn_w = sb("attn_w", [P, 4, D])
        self.attn_b = sb("attn_b", [P, 2])
        self.bv = sb("bv", [P, D])
        self.bo = sb("bo", [P, D])
        self.wr = sb("wr", [P, NE])
        self.br = sb("br", [P, NE])

    def expert_weights(self, ctx):
        sb = lambda name, shape: ctx.enter_context(self.nc.sbuf_tensor(name, shape, F32))
        self.w1 = sb("w1", [P, NE, FF])
        self.w2 = sb("w2", [P, NE, NG, D])
        self.b1 = sb("b1", [P, NE, FF])
        self.b2 = sb("b2", [P, NE, D])
        self.gamma, self.beta = sb("gamma", [P, D]), sb("beta", [P, D])
        self.gg, self.gb = sb("gg", [P, NB, D]), sb("gb", [P, NB, D])
        self.starts, self.tile_rows, self.pad_at = sb("starts", [P, NE]), sb("tile_rows", [P, TILES]), sb("pad_at", [P, 1])
        self.pad_rows = sb("pad_rows", [P, 2 * NE, ROW])

    def sems(self, names, counting_on=()):
        for n in names:
            self.S[n] = self.ctx.enter_context(self.nc.semaphore(n))
        for n in counting_on:
            old, stands_at = self.retired.pop(0) if self.retired else (None, 0)
            self.S[n] = self.S[old] if old else self.ctx.enter_context(self.nc.semaphore(n))
            self.base[n] = stands_at

    def wait(self, e, name, n):
        if not isinstance(n, int) or n > 0:
            e.wait_ge(self.S[name], n + self.base[name] if name in self.base else n)

    def alone(self, e, s):
        if not isinstance(s, int):
            e.nop(nofuse=True)


def bc3(ap, n, m):
    return ap.rearrange("p (h o) -> p h o", o=1).broadcast_to([P, n, m])


def conditioning(nc, k, a, ctx, spare):
    x, ident, ones, mod, rows0, gate_rows = k.x, k.ident, k.ones, k.mod, k.rows0, k.gate_rows
    bank, S = k.bank, k.S
    k.sems(("c_in", "x_in", "aw_in", "c_tanh", "c_dve", "c_mm", "c_mod", "c_gate", "c_row_mm", "c_ev_a", "c_ev_d", "c_set"))
    sb = lambda name, shape, dt=F32: ctx.enter_context(nc.sbuf_tensor(name, shape, dt))
    cT = sb("cT", [P, 2 * NB])
    cu = sb("cu", [P, 2 * NB])
    free = k.h_all[:].rearrange("p b t -> p (b t)")
    W = 2 * 6 * D
    wmod = free[:, 0:W].rearrange("p (l c) -> p l c", l=2)
    mrow = free[0:NB, W:2 * W].rearrange("p (l i d) -> p l i d", l=2, i=6)
    sign, size = (free[0:NB, 2 * W + i * 4 * D:2 * W + (i + 1) * 4 * D].rearrange("p (l i d) -> p l i d", l=2, i=2) for i in range(2))
    pick = spare[0:NB, :].rearrange("p (b m) -> p b m", b=NB)

    def start_sp(sp):
        for dst, key in ((cT[:], "cT"), (wmod, "wmod"), (pick, "pick"), (ident[:], "ident")):
            sp.dma_start(dst, a[key]).then_inc(S["c_in"], 16)
        sp.dma_start(x[:], a["x"].rearrange("b (c p) d -> p (b c) d", p=P)).then_inc(S["x_in"], 16)
        for dst, key in ((k.attn_w, "attn_w"), (k.attn_b, "attn_b"), (k.bv, "bv"), (k.bo, "bo"), (k.wr, "wr"), (k.br, "br"), (k.iota, "iota")):
            sp.dma_start(dst[:], a[key]).then_inc(S["aw_in"], 16)

    def start_pool(pool):
        nc.gpsimd.memset(k.half_neg[:], -0.5)
        nc.gpsimd.memset(k.eps[:], EPS)
        nc.gpsimd.memset(ones[:], 1.0).then_inc(S["c_set"], 1)
        pool.wait_ge(S["c_set"], 1)

    def start_act(act):
        ac = nc.scalar
        act.wait_ge(S["c_in"], 64)
        ac.activation(cu[:], cT[:], ACT.Tanh, scale=0.5).then_inc(S["c_tanh"], 1)
        act.wait_ge(S["c_mm"], 1)
        for h in range(4):
            ac.activation(mrow[:, h // 2, 3 * (h % 2):3 * (h % 2) + 3, :].rearrange("b k d -> b (k d)"), bank[1 + h][0:NB, 0:3 * D],
                          ACT.Copy).then_inc(S["c_mod"], 1)
        for b in range(NB):
            act.wait_ge(S["c_row_mm"], 2 * b + 2)
            src = bank[2 + 2 * (b % 3)]
            ac.activation(gate_rows[:, 1, b, :], src[:, 0:D], ACT.Copy)
            ac.activation(k.moe_rows[:, b].rearrange("p k d -> p (k d)"), src[:, D:3 * D], ACT.Copy)
            ac.activation(gate_rows[:, 2, b, :], src[:, 3 * D:4 * D], ACT.Copy).then_inc(S["c_ev_a"], 1)

    def start_dve(dve):
        v = nc.vector
        n = [0]

        def step(ins):
            n[0] += 1
            ins.then_inc(S["c_dve"], 1)
            dve.wait_ge(S["c_dve"], n[0])

        dve.wait_ge(S["c_in"], 64)
        dve.wait_ge(S["c_tanh"], 1)
        step(v.tensor_scalar(cT[:], cT[:], 0.5, None, ALU.mult))
        step(v.scalar_tensor_tensor(out=cu[:], in0=cu[:], scalar=1.0, in1=cT[:], op0=ALU.add, op1=ALU.mult))
        dve.wait_ge(S["c_mod"], 4)
        gates = mrow[:, :, 2::3, :]
        step(v.tensor_scalar(sign, gates, 0.0, 2.0, ALU.is_ge, ALU.mult))
        step(v.tensor_scalar(size, gates, -1.0, None, ALU.mult))
        step(v.tensor_tensor(size, size, gates, ALU.max))
        step(v.tensor_scalar(size, size, 0.25, None, ALU.max))
        step(v.scalar_tensor_tensor(out=gates, in0=sign, scalar=1.0, in1=size, op0=ALU.subtract, op1=ALU.mult))
        step(v.tensor_scalar(mrow[:, :, 1::3, :], mrow[:, :, 1::3, :], 1.0, None, ALU.add))
        v.tensor_copy(mod[:].rearrange("p l k b -> p (l k b)"), bank[0][:, 0:12 * NB]).then_inc(S["c_gate"], 1)
        dve.wait_ge(S["c_gate"], 1)
        for l in range(2):
            for i in (1, 4):
                step(v.tensor_scalar(mod[:, l, i, :], mod[:, l, i, :], 1.0, None, ALU.add))
        for b in range(NB):
            dve.wait_ge(S["c_row_mm"], 2 * b + 1)
            src = bank[1 + 2 * (b % 3)]
            v.tensor_copy(rows0[:, b].rearrange("p k d -> p (k d)"), src[:, 0:3 * D])
            v.tensor_copy(gate_rows[:, 0, b, :], src[:, 3 * D:4 * D]).then_inc(S["c_ev_d"], 1)

    def start_pe(pe):
        t_ = nc.tensor
        pe.wait_ge(S["c_in"], 64)
        pe.wait_ge(S["c_dve"], 2)
        for h in range(4):
            t_.matmul(bank[1 + h][0:NB, 0:3 * D], cu[:, (h // 2) * NB:(h // 2 + 1) * NB], wmod[:, h // 2, 3 * (h % 2) * D:3 * (h % 2 + 1) * D],
                      start=True, stop=True)
        for l in range(2):
            for i in range(6):
                mm = t_.matmul(bank[0][:, (l * 6 + i) * NB:(l * 6 + i + 1) * NB], wmod[:, l, i * D:(i + 1) * D],
                               cu[:, l * NB:(l + 1) * NB], start=True, stop=True)
        mm.then_inc(S["c_mm"], 1)
        pe.wait_ge(S["c_dve"], 8)
        for b in range(NB):
            if b >= 3:
                pe.wait_ge(S["c_ev_d"], b - 2)
                pe.wait_ge(S["c_ev_a"], b - 2)
            lo, hi = bank[1 + 2 * (b % 3)], bank[2 + 2 * (b % 3)]
            t_.matmul(lo[:, 0:3 * D], pick[:, b, :], mrow[:, 0, 0:3, :].rearrange("b k d -> b (k d)"), start=True, stop=True)
            t_.matmul(lo[:, 3 * D:4 * D], pick[:, b, :], mrow[:, 0, 5, :], start=True, stop=True).then_inc(S["c_row_mm"], 1)
            t_.matmul(hi[:], pick[:, b, :], mrow[:, 1, 2:6, :].rearrange("b k d -> b (k d)"), start=True, stop=True).then_inc(S["c_row_mm"], 1)
    return start_sp, start_pool, start_act, start_dve, start_pe


def mixer(nc, chip, a):
    x, h_all, ident, mod, ones, lg, ix, rows0, bank, S = (
        chip.x, chip.h_all, chip.ident, chip.mod, chip.ones, chip.lg, chip.ix, chip.rows0, chip.bank, chip.S)
    half_neg, eps, wait, alone = chip.half_neg[:, 0:1], chip.eps[:, 0:1], chip.wait, chip.alone
    with ExitStack() as ctx:
        def sb(name, shape, dt=F32):
            return ctx.enter_context(nc.sbuf_tensor(name, shape, dt))

        wc_hi = sb("wc_hi", [P, NTAP, SEQ], F32R)
        wc_lo = sb("wc_lo", [P, NTAP, SEQ], F32R)
        wz = sb("wz", [P, DI + NH])
        wz_hi = sb("wz_hi", [P, DI + NH], F32R)
        wz_lo = sb("wz_lo", [P, DI + NH], F32R)
        conv_b = sb("conv_b", [P, 4])
        hconv_b = sb("hconv_b", [P, 4])
        dt_b = sb("dt_b", [P, NH])
        a_neg = sb("a_neg", [P, NC * NH])
        a_log = sb("a_log", [P, NC * NH])
        d_bc = sb("d_bc", [P, DI])
        norm_w = sb("norm_w", [P, 2])
        wo = sb("wo", [P, 2, D])
        wo8 = sb("wo8", [P, NB, 2, D])
        res_g = sb("res_g", [P, NB, D])
        res_b = sb("res_b", [P, NB, D])
        gw = sb("gw", [P, NE])
        ident4 = sb("ident4", [P, NC * P])
        sel = sb("sel", [16, 16 * P])
        sel127 = sb("sel127", [P, P])
        zero16 = sb("zero16", [16, P])

        start_sp, start_pool, start_act, start_dve, start_pe = conditioning(
            nc, chip, a, ctx, res_b[:].rearrange("p b d -> p (b d)"))

        st1 = sb("st1", [P, 2, 6]); mv1 = sb("mv1", [P, 2, 2]); ve1 = sb("ve1", [P, 2, 1]); rs1 = sb("rs1", [P, 2, 1])
        st2 = sb("st2", [P, 2, 6]); mv2 = sb("mv2", [P, 2, 2]); ve2 = sb("ve2", [P, 2, 1]); rs2 = sb("rs2", [P, 2, 1])
        xn1 = sb("xn1", [P, 2, D]); xn2 = sb("xn2", [P, 2, D])
        rt1 = sb("rt1", [P, 2, D]); rt2 = sb("rt2", [P, 2, D])
        h_new = sb("h_new", [P, SEQ])
        h_hi = sb("h_hi", [P, 4 + SEQ], F32R)
        h_lo = sb("h_lo", [P, 4 + SEQ], F32R)
        cv = sb("cv", [P, 2, 4, SEQ])
        ct = sb("ct", [P, 2, 4, SEQ])
        cwb, wstage = cv[:, 0], ct[:, 0]
        zu = sb("zu", [P, 2, DI]); zt = sb("zt", [P, 2, DI])
        zs = sb("zs", [P, 2, NC, DI])
        dtr = sb("dtr", [P, NC * NH]); dta = sb("dta", [P, NC * NH]); dte = sb("dte", [P, NC * NH]); dtl = sb("dtl", [P, NC * NH])
        dt = sb("dt", [P, 2, NC * NH]); dax = sb("dax", [P, NC * NH]); da = sb("da", [P, NC * NH])
        da_t = sb("da_t", [16, 2, P]); cum_t = sb("cum_t", [16, P])
        cum = sb("cum", [P, 2, NC * NH]); tot = sb("tot", [P, 2, NC * NH])
        xc = sb("xc", [P, 2, 4, P])
        xb = sb("xb", [P, 2, 3 * P])
        lt = sb("lt", [P, 2, 4 * P]); mt = sb("mt", [P, 2, 4 * P])
        xdt = sb("xdt", [P, 2, DI]); xdw = sb("xdw", [P, 2, DI]); xd = sb("xd", [P, 2, DI])
        state = sb("state", [P, DI]); state_d = sb("state_d", [P, DI])
        y1 = sb("y1", [P, DI]); y2 = sb("y2", [P, DI]); y3 = sb("y3", [P, DI])
        yz = sb("yz", [P, 2, DI]); ysq = sb("ysq", [P, DI]); ss = sb("ss", [P, 2, 1]); sse = sb("sse", [P, 2, 1]); rr = sb("rr", [P, 2, 1])
        yt = sb("yt", [P, 2, DI])
        hc = sb("hc", [P, 2, P])
        lgc = sb("lgc", [P, 2, NE]); mx = sb("mx", [P, 2, NE]); mi = sb("mi", [P, 2, NE], U32)

        chip.sems((
            "w_in", "set_pool", "set_dve", "set_act",
            "pe_slot", "act_slot", "dve_slot", "pool_slot",
            "ln1_stats", "ln1_mv", "ln1_ve", "ln1_rs", "ln1_xn", "res_1", "res_2", "h_staged", "h_split", "h_split_hi",
            "f_mm", "f_v", "f_t", "z_mm", "z_act", "z_dt", "z_s",
            "d_abs", "d_exp", "d_ln", "d_dt", "d_dta", "d_da", "d_tr", "d_tz", "d_scan", "d_tr2", "d_cum", "d_mm", "d_tot",
            "s_xc", "s_tr", "s_g", "s_bc", "s_xb", "s_lt", "s_mt", "s_xdt", "s_xdw", "s_xd",
            "s_ymm", "s_smm", "s_sd", "s_state", "s_y1", "s_y2", "s_y3", "s_yz", "s_ss", "s_sse", "s_rr",
            "t_mm", "t_y", "t_h2", "o_mm", "o_x", "ln2_stats", "ln2_mv", "ln2_ve", "ln2_rs", "ln2_xn",
            "r_mm", "r_lg", "r_mx", "r_mi"))
        block = ctx.enter_context(nc.Block())

        DVE_SETUP, POOL_SETUP = 3, 29
        FIRST, LAST = -9, NT + 3

        def slots(e, body):
            for s in range(FIRST, NC):
                body(s, s // NC, s % NC, lambda lag: 0 <= s - lag < NT)
            with e.Fori(1, NB - 3) as b:
                for c in range(NC):
                    body(b * NC + c, b, c, lambda lag: True)
            for s in range((NB - 3) * NC, LAST):
                body(s, s // NC, s % NC, lambda lag: 0 <= s - lag < NT)

        def slot_begins(e, s):
            for name in ("pe_slot", "act_slot", "dve_slot", "pool_slot"):
                wait(e, name, s - 2 - FIRST + 1)

        def hv(ap):
            return ap.rearrange("p (h o) -> p h o", h=NH)

        def bc3(ap, n, m):
            return ap.rearrange("p (h o) -> p h o", o=1).broadcast_to([P, n, m])

        @block.sync
        def _(sp):
            start_sp(sp)
            for dst, key in ((wstage[:, 0, :], "w_xbc"), (cwb, "conv_w"), (wz[:], "w_zdt"), (conv_b[:], "conv_b"), (dt_b[:], "dt_b"),
                             (a_log[:], "a_log"), (d_bc[:], "d_bc"), (norm_w[:], "norm_w"), (wo[:], "w_out"),
                             (gw[:], "gate_w"), (ident4[:], "ident4"), (sel[:], "sel"), (sel127[:], "sel127")):
                sp.dma_start(dst, a[key]).then_inc(S["w_in"], 16)
            sp.wait_ge(S["w_in"], 16 * 13)
            sp.wait_ge(S["aw_in"], 16 * 7)

        @block.gpsimd
        def _(pool):
            start_pool(pool)
            g = nc.gpsimd
            n = [0]

            def step(ins):
                n[0] += 1
                ins.then_inc(S["set_pool"], 1)
                pool.wait_ge(S["set_pool"], n[0])

            step(g.memset(zero16[:], 0.0))
            step(g.memset(da_t[:, :, 0:1], 0.0))
            step(g.memset(h_hi[:, 0:4].bitcast(F32), 0.0))
            step(g.memset(h_lo[:, 0:4].bitcast(F32), 0.0))
            pool.wait_ge(S["w_in"], 16 * 13)
            for k in range(NTAP):
                step(g.tensor_tensor(cwb[:, k, :], cwb[:, k, :], wstage[:, 0, :], ALU.mult))
                step(g.tensor_copy(wc_hi[:, k, :], cwb[:, k, :]))
                step(g.tensor_tensor(wc_lo[:, k, :], cwb[:, k, :], wc_hi[:, k, :].bitcast(F32), ALU.subtract))
            step(g.tensor_copy(wz_hi[:], wz[:]))
            step(g.tensor_tensor(wz_lo[:], wz[:], wz_hi[:].bitcast(F32), ALU.subtract))
            step(g.tensor_scalar(hconv_b[:], conv_b[:], 0.5, None, ALU.mult))
            for k in range(2):
                step(g.tensor_scalar(wo[:, k, :], wo[:, k, :], norm_w[:, k:k + 1], None, ALU.mult))
            pool.wait_ge(S["c_ev_d"], NB)
            for b in range(NB):
                step(g.tensor_tensor(wo8[:, b], wo[:], rows0[:, b, 2, :].rearrange("p (o d) -> p o d", o=1).broadcast_to([P, 2, D]), ALU.mult))
            assert n[0] == POOL_SETUP, n[0]

            def body(s, b, c, has):
                slot_begins(pool, s)
                if has(-9):
                    t, p, ba = s + 9, (c + 1) % 2, b + 2 if c < 3 else b + 3
                    wait(pool, "ln1_mv", t + 1)
                    g.tensor_tensor(ve1[:, p, :], mv1[:, p, 1:2], eps, ALU.add).then_inc(S["ln1_ve"], 1)
                    wait(pool, "ln1_ve", t + 1)
                    g.tensor_tensor(rs1[:, p, :], ve1[:, p, :], half_neg, ALU.pow).then_inc(S["ln1_rs"], 1)
                if has(1):
                    cs = (c - 1) % 4
                    if cs in (1, 2):
                        wait(pool, "s_state", s - 1)
                        alone(pool, s)
                        q = b % 2
                        g.tensor_tensor(hv(state_d[:]), hv(state[:]),
                                        bc3(tot[:, q, cs * NH:cs * NH + NH], NH, HD), ALU.mult).then_inc(S["s_sd"], 1)
                    else:
                        pool.drain().then_inc(S["s_sd"], 1)
                if has(0):
                    p, q = c % 2, b % 2
                    wait(pool, "s_xb", s + 1)
                    wait(pool, "s_smm", s - 1)
                    wait(pool, "s_y3", s - 1)
                    g.tensor_tensor(xd[:, p, :], xb[:, p, 0:DI], d_bc[:], ALU.mult).then_inc(S["s_xd"], 1)
                    g.tensor_tensor(hv(xdt[:, p, :]), hv(xb[:, p, 0:DI]), bc3(dt[:, q, c * NH:c * NH + NH], NH, HD),
                                    ALU.mult).then_inc(S["s_xdt"], 1)
                    wait(pool, "s_xdt", s + 1)
                    wait(pool, "s_lt", s + 1)
                    g.tensor_tensor(hv(xdw[:, p, :]), hv(xdt[:, p, :]),
                                    lt[:, p, :].rearrange("p (h i) -> p h i", h=NH)[:, :, P - 1:P].broadcast_to([P, NH, HD]),
                                    ALU.mult).then_inc(S["s_xdw"], 1)
                if has(-9):
                    wait(pool, "ln1_xn", t + 1)
                    alone(pool, s)
                    g.tensor_tensor(rt1[:, (c + 1) % 2, :], xn1[:, (c + 1) % 2, :], res_g[:, ba, :], ALU.mult).then_inc(S["res_1"], 1)
                if has(2):
                    t2, p = s - 2, c % 2
                    wait(pool, "ln2_mv", t2 + 1)
                    g.tensor_tensor(ve2[:, p, :], mv2[:, p, 1:2], eps, ALU.add).then_inc(S["ln2_ve"], 1)
                    wait(pool, "ln2_ve", t2 + 1)
                    g.tensor_tensor(rs2[:, p, :], ve2[:, p, :], half_neg, ALU.pow).then_inc(S["ln2_rs"], 1)
                if has(-9):
                    wait(pool, "res_1", t + 1)
                    alone(pool, s)
                    g.tensor_tensor(rt2[:, (c + 1) % 2, :], rt1[:, (c + 1) % 2, :], res_b[:, ba, :], ALU.add).then_inc(S["res_2"], 1)
                if has(1):
                    t1, p = s - 1, (c + 1) % 2
                    wait(pool, "s_ss", t1 + 1)
                    wait(pool, "o_x", s - 2)
                    g.tensor_tensor(sse[:, p, :], ss[:, p, :], eps, ALU.add).then_inc(S["s_sse"], 1)
                    wait(pool, "s_sse", t1 + 1)
                    g.tensor_tensor(rr[:, p, :], sse[:, p, :], half_neg, ALU.pow).then_inc(S["s_rr"], 1)
                if has(-9):
                    wait(pool, "res_2", t + 1)
                    alone(pool, s)
                    g.tensor_tensor(x[:, t, :], x[:, t, :], rt2[:, (c + 1) % 2, :], ALU.add)
                if has(3):
                    t3, p = s - 3, (c + 1) % 2
                    bb = b if c == 3 else b - 1
                    cc = (c + 1) % 4
                    wait(pool, "t_h2", t3 + 1)
                    wait(pool, "r_lg", t3 + 1)
                    alone(pool, s)
                    g.tensor_copy(h_all[:, bb, cc * P:cc * P + P], hc[:, p, :])
                    g.tensor_copy(lg[:, t3, :], lgc[:, p, :])
                pool.drain().then_inc(S["pool_slot"], 1)

            slots(pool, body)

        @block.scalar
        def _(act):
            start_act(act)
            ac = nc.scalar
            act.wait_ge(S["w_in"], 16 * 13)
            act.wait_ge(S["c_dve"], 12)
            ac.activation(a_neg[:], a_log[:], ACT.Exp).then_inc(S["set_act"], 1)

            def body(s, b, c, has):
                slot_begins(act, s)
                q1 = (b + 1) % 2
                if has(-4) and c < 2:
                    k = 2 * c
                    wait(act, "z_s", (b + 1) * 4 + k - 1)
                    wait(act, "z_mm", (b + 1) * 4 + k + 1)
                    ac.activation(zu[:, 0, :], bank[0][:, 0:DI], ACT.Copy, scale=0.5)
                    ac.activation(zt[:, 0, :], bank[0][:, 0:DI], ACT.Tanh, scale=0.5).then_inc(S["z_act"], 1)
                if has(-4):
                    wait(act, "f_mm", s + 4 + 1)
                    wait(act, "s_xc", b * 4)
                    alone(act, s)
                    ac.activation(cv[:, q1, c, :], bank[1][:], ACT.Identity, scale=0.5, bias=hconv_b[:, c:c + 1]).then_inc(S["f_v"], 1)
                    ac.activation(ct[:, q1, c, :], bank[1][:], ACT.Tanh, scale=0.5, bias=hconv_b[:, c:c + 1]).then_inc(S["f_t"], 1)
                tr = [has(-8), has(2), has(3)]
                if any(tr):
                    wait(act, "t_mm", s - FIRST + 1)
                if tr[0] and c == 0:
                    wait(act, "h_split", b + 2)
                if tr[1]:
                    ac.activation(yt[:, c % 2, :], bank[7][:, P:P + DI], ACT.Copy).then_inc(S["t_y"], 1)
                if tr[0]:
                    ac.activation(h_new[:, c * P:c * P + P], bank[7][:, 0:P], ACT.Identity,
                                  scale=mod[:, 0, 1, bass.ds(b + 2, 1)], bias=mod[:, 0, 0, bass.ds(b + 2, 1)]).then_inc(S["h_staged"], 1)
                if tr[0] and c == 3:
                    wait(act, "h_staged", s + 9)
                    ac.activation(h_hi[:, 3:3 + SEQ], h_new[:], ACT.Copy).then_inc(S["h_split_hi"], 1)
                if tr[2]:
                    bb = b if c == 3 else b - 1
                    ac.activation(hc[:, (c + 1) % 2, :], bank[7][:, 3 * P:4 * P], ACT.Identity,
                                  scale=mod[:, 0, 4, bass.ds(bb, 1)], bias=mod[:, 0, 3, bass.ds(bb, 1)]).then_inc(S["t_h2"], 1)
                if has(0):
                    wait(act, "s_tr", s + 1)
                    wait(act, "s_smm", s - 1)
                    ac.activation(xb[:, c % 2, :], bank[2][:, 0:3 * P], ACT.Copy).then_inc(S["s_xb"], 1)
                if has(-4) and c < 2:
                    k = 2 * c + 1
                    wait(act, "z_s", (b + 1) * 4 + k - 1)
                    wait(act, "z_mm", (b + 1) * 4 + k + 1)
                    ac.activation(zu[:, 1, :], bank[0][:, 0:DI], ACT.Copy, scale=0.5)
                    ac.activation(zt[:, 1, :], bank[0][:, 0:DI], ACT.Tanh, scale=0.5).then_inc(S["z_act"], 1)
                if has(-4) and c == 2:
                    wait(act, "z_dt", (b + 1) * 4 + 4)
                    ac.activation(dta[:], dtr[:], ACT.Abs).then_inc(S["d_abs"], 1)
                    wait(act, "d_abs", b + 2)
                    ac.activation(dte[:], dta[:], ACT.Exp, scale=-1.0).then_inc(S["d_exp"], 1)
                    wait(act, "d_exp", b + 2)
                    ac.activation(dtl[:], dte[:], ACT.Ln, bias=1.0).then_inc(S["d_ln"], 1)
                    wait(act, "d_dta", b + 2)
                    ac.activation(da[:], dax[:], ACT.Exp).then_inc(S["d_da"], 1)
                if has(1):
                    wait(act, "s_yz", s)
                    wait(act, "s_ss", s - 1)
                    ac.activation(ysq[:], yz[:, (c + 1) % 2, :], ACT.Square, scale=1.0 / 16, accum_out=ss[:, (c + 1) % 2, :]).then_inc(S["s_ss"], 1)
                act.drain().then_inc(S["act_slot"], 1)

            slots(act, body)

        @block.vector
        def _(dve):
            start_dve(dve)
            dve.wait_ge(S["x_in"], 16)
            dve.wait_ge(S["c_ev_d"], NB)
            dve.wait_ge(S["c_row_mm"], 2 * NB)
            dve.wait_ge(S["c_row_mm"], 2 * NB)
            dve.wait_ge(S["c_row_mm"], 2 * NB)
            dve.wait_ge(S["c_row_mm"], 2 * NB)
            dve.wait_ge(S["c_row_mm"], 2 * NB)
            dve.wait_ge(S["c_row_mm"], 2 * NB)
            dve.wait_ge(S["c_row_mm"], 2 * NB)
            dve.wait_ge(S["c_row_mm"], 2 * NB)
            dve.wait_ge(S["c_row_mm"], 2 * NB)
            dve.wait_ge(S["c_dve"], 12)
            v = nc.vector
            n = [0]

            def step(ins):
                n[0] += 1
                ins.then_inc(S["set_dve"], 1)
                dve.wait_ge(S["set_dve"], n[0])

            step(v.tensor_tensor(res_g[:], rows0[:, :, 1, :], rows0[:, :, 2, :], ALU.mult))
            step(v.tensor_tensor(res_b[:], rows0[:, :, 0, :], rows0[:, :, 2, :], ALU.mult))
            dve.wait_ge(S["set_act"], 1)
            step(v.tensor_scalar(a_neg[:], a_neg[:], -1.0, None, ALU.mult))
            assert n[0] == DVE_SETUP, n[0]
            dve.wait_ge(S["set_pool"], POOL_SETUP)

            def count(n):
                return min(n, NT) if isinstance(n, int) else n

            def y_count(b, c):
                return 3 * b + c - 1 if c else 3 * b

            def body(s, b, c, has):
                slot_begins(dve, s)
                q1 = (b + 1) % 2
                p, pn = c % 2, (c + 1) % 2
                cs = (c - 1) % 4
                qs = b % 2 if c else (b + 1) % 2
                if has(-9):
                    v.bn_stats(st1[:, pn, :], x[:, s + 9, :]).then_inc(S["ln1_stats"], 1)
                wait(dve, "ln1_stats", count(s + 10))
                if has(0):
                    wait(dve, "f_t", b * 4 + 4)
                    wait(dve, "s_ymm", s - 1)
                    v.scalar_tensor_tensor(out=xc[:, p], in0=ct[:, b % 2, :, c * P:c * P + P], scalar=1.0,
                                           in1=cv[:, b % 2, :, c * P:c * P + P], op0=ALU.add, op1=ALU.mult).then_inc(S["s_xc"], 1)
                if has(-9):
                    v.bn_aggr(mv1[:, pn, :], st1[:, pn, :]).then_inc(S["ln1_mv"], 1)

                def z(i):
                    k = 2 * c + i
                    wait(dve, "z_act", (b + 1) * 4 + k + 1)
                    wait(dve, "s_yz", s - 1)
                    v.tensor_tensor(dtr[:, k * NH:k * NH + NH], bank[0][:, DI:DI + NH], dt_b[:], ALU.add).then_inc(S["z_dt"], 1)
                    v.scalar_tensor_tensor(out=zs[:, q1, k, :], in0=zt[:, i, :], scalar=1.0, in1=zu[:, i, :],
                                           op0=ALU.add, op1=ALU.mult).then_inc(S["z_s"], 1)

                if has(-4) and c < 2:
                    z(0)
                if has(-4) and c == 3:
                    wait(dve, "d_tr", b + 2)
                    alone(dve, s)
                    v.tensor_copy(da_t[:, q1, 1:P], bank[4][0:16, 257:384]).then_inc(S["d_tz"], 1)
                    v.tensor_tensor_scan(cum_t[:], bank[4][0:16, 256:384], zero16[:], 1.0, ALU.mult, ALU.add).then_inc(S["d_scan"], 1)
                if has(0):
                    wait(dve, "s_bc", s + 1)
                    v.tensor_tensor_scan(lt[:, p, :], bank[3][:], ident4[:], 0.0, ALU.mult, ALU.add).then_inc(S["s_lt"], 1)
                if has(-9):
                    wait(dve, "t_mm", s - 1 - FIRST + 1)
                    wait(dve, "ln1_rs", s + 10)
                    v.tensor_scalar(xn1[:, pn, :], x[:, s + 9, :], mv1[:, pn, 0:1], rs1[:, pn, :], ALU.subtract, ALU.mult).then_inc(S["ln1_xn"], 1)
                if has(0):
                    wait(dve, "s_lt", s + 1)
                    wait(dve, "s_g", s + 1)
                    wait(dve, "s_ymm", s - 1)
                    v.tensor_tensor(mt[:, p, :].rearrange("p (h i) -> p h i", h=NH), lt[:, p, :].rearrange("p (h i) -> p h i", h=NH),
                                    bank[6][:, DI:DI + P].rearrange("p (o i) -> p o i", o=1).broadcast_to([P, NH, P]),
                                    ALU.mult).then_inc(S["s_mt"], 1)
                if has(-8) and c == 3:
                    wait(dve, "h_split_hi", b + 3)
                    wait(dve, "f_mm", s + 4 + 1)
                    v.tensor_tensor(h_lo[:, 3:3 + SEQ], h_new[:], h_hi[:, 3:3 + SEQ].bitcast(F32), ALU.subtract).then_inc(S["h_split"], 1)
                if has(-4) and c < 2:
                    z(1)
                if has(-4) and c == 3:
                    wait(dve, "d_tr2", b + 2)
                    alone(dve, s)
                    v.tensor_copy(cum[:, q1, :], bank[4][:, 384:400]).then_inc(S["d_cum"], 1)
                if has(2):
                    wait(dve, "o_mm", s - 1)
                    wait(dve, "s_rr", s - 1)
                    v.scalar_tensor_tensor(out=x[:, s - 2, :], in0=bank[4][:, 0:P], scalar=rr[:, p, :], in1=x[:, s - 2, :],
                                           op0=ALU.mult, op1=ALU.add).then_inc(S["o_x"], 1)
                if has(1):
                    wait(dve, "s_smm", s)
                    wait(dve, "s_yz", s - 1)
                    wait(dve, "s_xd", s)
                    if cs:
                        alone(dve, s)
                        v.tensor_tensor(hv(y1[:]), hv(bank[5][:, DI:2 * DI]), bc3(cum[:, qs, cs * NH:cs * NH + NH], NH, HD), ALU.mult).then_inc(S["s_y1"], 1)
                    else:
                        v.tensor_tensor(y3[:], bank[5][:, 0:DI], xd[:, pn, :], ALU.add).then_inc(S["s_y3"], 1)
                wait(dve, "o_x", count(s - 1))
                if has(2):
                    alone(dve, s)
                    v.bn_stats(st2[:, p, :], x[:, s - 2, :]).then_inc(S["ln2_stats"], 1)
                if has(1):
                    wait(dve, "s_sd", s)
                    if cs in (1, 2):
                        v.tensor_tensor(state[:], state_d[:], bank[6][:, 0:DI], ALU.add).then_inc(S["s_state"], 1)
                    elif cs == 0:
                        wait(dve, "s_y3", s)
                        v.tensor_copy(state[:], bank[6][:, 0:DI]).then_inc(S["s_state"], 1)
                    if cs:
                        wait(dve, "s_y1", y_count(b, c))
                        v.tensor_tensor(y2[:], y1[:], bank[5][:, 0:DI], ALU.add).then_inc(S["s_y2"], 1)
                if has(-4) and c == 2:
                    wait(dve, "d_ln", b + 2)
                    v.scalar_tensor_tensor(out=dt[:, q1, :], in0=dtr[:], scalar=0.0, in1=dtl[:], op0=ALU.max, op1=ALU.add).then_inc(S["d_dt"], 1)
                wait(dve, "ln2_stats", count(s - 1))
                if has(2):
                    alone(dve, s)
                    v.bn_aggr(mv2[:, p, :], st2[:, p, :]).then_inc(S["ln2_mv"], 1)
                if has(1) and cs:
                    wait(dve, "s_y2", y_count(b, c))
                    v.tensor_tensor(y3[:], y2[:], xd[:, pn, :], ALU.add).then_inc(S["s_y3"], 1)
                if has(-4) and c == 3:
                    wait(dve, "d_mm", b + 2)
                    alone(dve, s)
                    v.tensor_copy(tot[:, q1, :], bank[4][:, 400:416]).then_inc(S["d_tot"], 1)
                if has(3):
                    wait(dve, "r_mm", s - 2)
                    v.tensor_copy(lgc[:, pn, :], bank[4][:, P:P + NE]).then_inc(S["r_lg"], 1)
                wait(dve, "r_lg", count(s - 2))
                if has(-4) and c == 2:
                    wait(dve, "d_dt", b + 2)
                    alone(dve, s)
                    v.tensor_tensor(dax[:], dt[:, q1, :], a_neg[:], ALU.mult).then_inc(S["d_dta"], 1)
                if has(1):
                    wait(dve, "s_y3", s)
                    wait(dve, "t_mm", s - 1 - FIRST + 1)
                    if isinstance(s, int):
                        v.tensor_tensor(yz[:, pn, :], y3[:], zs[:, qs, cs, :], ALU.mult).then_inc(S["s_yz"], 1)
                    else:
                        alone(dve, s)
                        v.tensor_tensor(yz[:, pn, :], y3[:], zs[:, qs, cs, :], ALU.mult).then_inc(S["s_yz"], 1)
                if has(3):
                    v.max(mx[:, pn, :], lgc[:, pn, :]).then_inc(S["r_mx"], 1)
                wait(dve, "r_mx", count(s - 2))
                wait(dve, "ln2_rs", count(s - 1))
                wait(dve, "t_mm", s - 1 - FIRST + 1)
                if has(2):
                    v.tensor_scalar(xn2[:, p, :], x[:, s - 2, :], mv2[:, p, 0:1], rs2[:, p, :], ALU.subtract, ALU.mult).then_inc(S["ln2_xn"], 1)
                if has(3):
                    v.max_index(mi[:, pn, :], mx[:, pn, :], lgc[:, pn, :]).then_inc(S["r_mi"], 1)
                if has(3):
                    wait(dve, "r_mi", s - 2)
                    v.tensor_copy(ix[:, s - 3, :], mi[:, pn, 0:2])
                if has(1) and cs == 3:
                    dve.drain().then_inc(S["s_state"], 1)
                dve.drain().then_inc(S["dve_slot"], 1)

            slots(dve, body)

        @block.tensor
        def _(pe):
            start_pe(pe)
            pe.wait_ge(S["c_ev_d"], NB)
            pe.wait_ge(S["c_ev_a"], NB)
            t_ = nc.tensor
            pe.wait_ge(S["set_dve"], DVE_SETUP)
            pe.wait_ge(S["set_pool"], POOL_SETUP)

            def split3(dst, l_hi, l_lo, r_hi, r_lo, first, last):
                t_.matmul(dst, l_hi, r_hi, start=first, stop=False)
                t_.matmul(dst, l_lo, r_hi, start=False, stop=False)
                return t_.matmul(dst, l_hi, r_lo, start=False, stop=last)

            def body(s, b, c, has):
                slot_begins(pe, s)
                p, pn = c % 2, (c + 1) % 2
                q, q1 = b % 2, (b + 1) % 2

                def z(i):
                    k = 2 * c + i
                    wait(pe, "z_dt", (b + 1) * 4 + k)
                    split3(bank[0][:, 0:DI + NH], h_hi[:, 3 + k * P:3 + k * P + P], h_lo[:, 3 + k * P:3 + k * P + P],
                           wz_hi[:], wz_lo[:], True, True).then_inc(S["z_mm"], 1)

                if has(-4) and c == 0:
                    wait(pe, "h_split", b + 2)
                if has(-4) and c < 2:
                    z(0)
                if has(-4):
                    wait(pe, "f_t", s + 4)
                    for k in range(NTAP):
                        mm = split3(bank[1][:], wc_hi[:, k, c * P:c * P + P], wc_lo[:, k, c * P:c * P + P],
                                    h_hi[:, k:k + SEQ], h_lo[:, k:k + SEQ], k == 0, k == NTAP - 1)
                    mm.then_inc(S["f_mm"], 1)
                if has(-8) or has(2) or has(3):
                    for name, n in (("h_staged", s + 8), ("t_y", s - 2), ("t_h2", s - 3)):
                        wait(pe, name, min(n, NT) if isinstance(n, int) else n)
                    if has(2):
                        wait(pe, "s_yz", s - 1)
                        for k in range(2):
                            mm = t_.transpose(bank[7][:, P + k * P:2 * P + k * P], yz[:, p, k * P:k * P + P], ident[:])
                    if has(3):
                        wait(pe, "ln2_xn", s - 2)
                        mm = t_.transpose(bank[7][:, 3 * P:4 * P], xn2[:, pn, :], ident[:])
                    if has(-8):
                        wait(pe, "ln1_xn", s + 9)
                        mm = t_.transpose(bank[7][:, 0:P], xn1[:, p, :], ident[:])
                    mm.then_inc(S["t_mm"], 1)
                else:
                    pe.drain().then_inc(S["t_mm"], 1)
                if has(-4) and c == 3:
                    wait(pe, "d_da", b + 2)
                    wait(pe, "r_lg", s - 4 + 1)
                    wait(pe, "o_x", s - 3 + 1)
                    t_.transpose(bank[4][0:16, 256:384], da[:], ident[:]).then_inc(S["d_tr"], 1)
                if has(0):
                    wait(pe, "s_xc", s + 1)
                    wait(pe, "s_xb", s)
                    wait(pe, "s_lt", s)
                    wait(pe, "d_tz", b + 1)
                    for k in range(3):
                        mm = t_.transpose(bank[2][:, k * P:k * P + P], xc[:, p, k, :], ident[:])
                    mm.then_inc(S["s_tr"], 1)
                    for h in range(NH):
                        mm = t_.matmul(bank[3][:, h * P:h * P + P], sel[:, (c * NH + h) * P:(c * NH + h + 1) * P], da_t[:, q, :],
                                       start=True, stop=True)
                    mm.then_inc(S["s_bc"], 1)
                    wait(pe, "s_mt", s)
                    wait(pe, "s_state", s - 1)
                    t_.matmul(bank[6][:, DI:DI + P], xc[:, p, 2, :], xc[:, p, 3, :], start=True, stop=True).then_inc(S["s_g"], 1)
                if has(-4) and c < 2:
                    z(1)
                if has(-4) and c == 3:
                    wait(pe, "d_scan", b + 2)
                    alone(pe, s)
                    t_.transpose(bank[4][:, 384:400], cum_t[:], ident[0:16, 0:16]).then_inc(S["d_tr2"], 1)
                if has(2):
                    wait(pe, "t_y", s - 2 + 1)
                    wait(pe, "r_lg", s - 4 + 1)
                    if has(-4) and c == 3:
                        wait(pe, "d_cum", b + 2)
                    for k in range(2):
                        mm = t_.matmul(bank[4][:, 0:P], yt[:, p, k * P:k * P + P], wo8[:, b - 1 if c < 2 else b, k, :], start=(k == 0), stop=(k == 1))
                    mm.then_inc(S["o_mm"], 1)
                if has(1):
                    cs = (c - 1) % 4
                    wait(pe, "s_mt", s)
                    wait(pe, "s_xdt", s)
                    wait(pe, "s_y3", s - 1)
                    for h in range(NH):
                        mm = t_.matmul(bank[5][:, h * HD:h * HD + HD], mt[:, pn, h * P:h * P + P], xdt[:, pn, h * HD:h * HD + HD],
                                       start=True, stop=True)
                    if cs:
                        wait(pe, "s_state", s - 1)
                        mm = t_.matmul(bank[5][:, DI:2 * DI], xc[:, pn, 3, :], state[:], start=True, stop=True)
                    mm.then_inc(S["s_ymm"], 1)
                    if cs < 3:
                        wait(pe, "s_xdw", s)
                        if has(0):
                            wait(pe, "s_mt", s + 1)
                        t_.matmul(bank[6][:, 0:DI], xb[:, pn, DI:DI + P], xdw[:, pn, :], start=True, stop=True).then_inc(S["s_smm"], 1)
                    else:
                        pe.drain().then_inc(S["s_smm"], 1)
                if has(-4) and c == 3:
                    wait(pe, "d_cum", b + 2)
                    if has(2):
                        wait(pe, "o_x", s - 2 + 1)
                    t_.matmul(bank[4][:, 400:416], sel127[:], cum[:, q1, :], start=True, stop=True).then_inc(S["d_mm"], 1)
                if has(3):
                    wait(pe, "t_h2", s - 3 + 1)
                    wait(pe, "r_lg", s - 3)
                    wait(pe, "o_x", s - 2 + 1 if has(2) else s - 3 + 1)
                    if has(-4) and c == 3:
                        wait(pe, "d_tot", b + 2)
                    t_.matmul(bank[4][:, P:P + NE], hc[:, pn, :], gw[:], start=True, stop=True).then_inc(S["r_mm"], 1)
                pe.drain().then_inc(S["pe_slot"], 1)

            slots(pe, body)
    chip.retired = [(n, NT) for n in (
        "ln1_stats", "ln1_mv", "ln1_ve", "ln1_rs", "ln1_xn", "res_1", "res_2", "h_staged", "f_mm", "f_t", "z_mm", "z_act", "z_dt", "z_s",
        "s_xc", "s_tr", "s_g", "s_bc", "s_xb", "s_lt", "s_mt", "s_xdt", "s_xdw", "s_xd", "s_ymm", "s_smm", "s_sd", "s_y3", "s_yz",
        "s_ss", "s_sse", "s_rr", "t_y", "t_h2", "o_mm", "o_x", "ln2_stats", "ln2_mv", "ln2_ve", "ln2_rs", "ln2_xn",
        "r_mm", "r_lg", "r_mx", "r_mi")]


def l0_experts(nc, k, a):
    x, h_all, ones, lg, ix, bank, S = k.x, k.h_all, k.ones, k.lg, k.ix, k.bank, k.S
    wait, alone = k.wait, k.alone
    k.sems(("g_step", "g_cnt", "g_flag", "g_in", "g_sh", "g_exp", "g_comb", "g_hmm", "g_hev", "g_ymm", "g_acc", "g_gated", "g_x"))
    with ExitStack() as ctx:
        sb = lambda name, shape, dt=F32: ctx.enter_context(nc.sbuf_tensor(name, shape, dt))
        m0 = sb("g_m0", [P, NT, NE]); m1 = sb("g_m1", [P, NT, NE])
        mine = sb("g_mine", [P, NE]); keep = sb("g_keep", [P, NE]); any_kept = sb("g_any", [P, 1]); flag = sb("g_flagi", [P, 1], I32)
        peak = sb("g_peak", [P, NT]); ex = sb("g_ex", [P, NT, NE]); total = sb("g_total", [P, NT])
        w1 = sb("g_w1", [P, NE, D]); w2 = sb("g_w2", [P, NE, D]); b1 = sb("g_b1", [P, NE]); b2 = sb("g_b2", [1, NE, D])
        ht = sb("g_ht", [P, 2, SEQ]); acc = sb("g_acc_sb", [P, 2, NC, D]); gated = sb("g_gated_sb", [P, NC, D])
        block = ctx.enter_context(nc.Block())

        def any_expert_kept(e):
            e.wait_ge(S["g_flag"], 1)
            return e.value_load(flag[0:1, 0:1], min_val=0, max_val=1) != 0

        @block.vector
        def _(dve):
            v = nc.vector
            n = [0]

            def step(ins):
                n[0] += 1
                ins.then_inc(S["g_step"], 1)
                dve.wait_ge(S["g_step"], n[0])

            iot = k.iota[:].rearrange("p (o e) -> p o e", o=1).broadcast_to([P, NT, NE])
            step(v.tensor_tensor(m0[:], ix[:, :, 0:1].broadcast_to([P, NT, NE]), iot, ALU.is_equal))
            step(v.tensor_tensor(m1[:], ix[:, :, 1:2].broadcast_to([P, NT, NE]), iot, ALU.is_equal))
            step(v.tensor_tensor(m0[:], m0[:], m1[:], ALU.add))
            step(v.tensor_reduce(mine[:], m0[:].rearrange("p t e -> p e t"), AX.X, ALU.add))
            dve.wait_ge(S["g_cnt"], 1)
            step(v.tensor_scalar(keep[:], bank[0][:, 0:NE], float(CAP), None, ALU.is_le))
            step(v.tensor_reduce(any_kept[:], keep[:], AX.X, ALU.max))
            v.tensor_copy(flag[:], any_kept[:]).then_inc(S["g_flag"], 1)
            with dve.If(any_expert_kept(dve)):
                step(v.tensor_reduce(peak[:], lg[:], AX.X, ALU.max))
                v.tensor_tensor(ex[:], lg[:], bc3(peak[:], NT, NE), ALU.subtract).then_inc(S["g_sh"], 1)
                dve.wait_ge(S["g_exp"], 1)
                step(v.tensor_reduce(total[:], ex[:], AX.X, ALU.add))
                step(v.reciprocal(total[:], total[:]))
                step(v.tensor_tensor(ex[:], ex[:], bc3(total[:], NT, NE), ALU.mult))
                step(v.tensor_tensor(ex[:], ex[:], m0[:], ALU.mult))
                v.tensor_tensor(ex[:], ex[:], keep[:].rearrange("p (o e) -> p o e", o=1).broadcast_to([P, NT, NE]), ALU.mult).then_inc(S["g_comb"], 1)
                dve.wait_ge(S["g_comb"], 1)
                def sequence(b):
                    for e in range(NE):
                        wait(dve, "g_ymm", b * NE + e + 1)
                        if e == 0:
                            wait(dve, "g_gated", b)
                        wait(dve, "g_acc", (b * NE + e) * NC)
                        for c in range(NC):
                            w = ex[:, b * NC + c, e:e + 1]
                            y = bank[4 + e % 2][:, c * P:c * P + P]
                            if e == 0:
                                v.tensor_scalar(acc[:, 1, c, :], y, w, None, ALU.mult).then_inc(S["g_acc"], 1)
                            else:
                                v.scalar_tensor_tensor(out=acc[:, (e + 1) % 2, c, :], in0=y, scalar=w, in1=acc[:, e % 2, c, :],
                                                       op0=ALU.mult, op1=ALU.add).then_inc(S["g_acc"], 1)

                sequence(0)
                with dve.Fori(1, NB) as b:
                    sequence(b)

        @block.sync
        def _(sp):
            with sp.If(any_expert_kept(sp)):
                for dst, key in ((w1, "g_w1"), (w2, "g_w2"), (b1, "g_b1"), (b2, "g_b2")):
                    sp.dma_start(dst[:], a[key]).then_inc(S["g_in"], 16)
                sp.wait_ge(S["g_in"], 64)

        @block.gpsimd
        def _(pool):
            g = nc.gpsimd
            with pool.If(any_expert_kept(pool)):
                def sequence(b):
                    wait(pool, "g_acc", (b + 1) * NE * NC)
                    wait(pool, "g_x", b)
                    alone(pool, b)
                    for c in range(NC):
                        ins = g.tensor_tensor(gated[:, c, :], acc[:, 0, c, :], k.gate_rows[:, 0, b, :], ALU.mult)
                    ins.then_inc(S["g_gated"], 1)
                    wait(pool, "g_gated", b + 1)
                    alone(pool, b)
                    g.tensor_tensor(x[:, bass.ds(b * NC, NC), :], x[:, bass.ds(b * NC, NC), :], gated[:], ALU.add).then_inc(S["g_x"], 1)

                sequence(0)
                with pool.Fori(1, NB) as b:
                    sequence(b)

        @block.scalar
        def _(act):
            ac = nc.scalar
            with act.If(any_expert_kept(act)):
                act.wait_ge(S["g_sh"], 1)
                ac.activation(ex[:], ex[:], ACT.Exp).then_inc(S["g_exp"], 1)
                act.wait_ge(S["g_in"], 64)
                def sequence(b):
                    for e in range(NE):
                        wait(act, "g_hmm", b * NE + e + 1)
                        alone(act, b)
                        ac.activation(ht[:, e % 2, :], bank[e % 2][:], ACT.Relu, bias=b1[:, e:e + 1]).then_inc(S["g_hev"], 1)

                sequence(0)
                with act.Fori(1, NB) as b:
                    sequence(b)

        @block.tensor
        def _(pe):
            t_ = nc.tensor
            pe.wait_ge(S["g_step"], 4)
            t_.matmul(bank[0][:, 0:NE], ones[:], mine[:], start=True, stop=True).then_inc(S["g_cnt"], 1)
            with pe.If(any_expert_kept(pe)):
                pe.wait_ge(S["g_in"], 64)

                def hidden(b, e):
                    wait(pe, "g_hev", b * NE + e)
                    t_.matmul(bank[e % 2][:], w1[:, e, :], h_all[:, b, :], start=True, stop=True).then_inc(S["g_hmm"], 1)

                def sequence(b):
                    hidden(b, 0)
                    for e in range(NE):
                        wait(pe, "g_hev", b * NE + e + 1)
                        wait(pe, "g_acc", (b * NE + e) * NC)
                        for c in range(NC):
                            y = bank[4 + e % 2][:, c * P:c * P + P]
                            t_.matmul(y, ht[:, e % 2, c * P:c * P + P], w2[:, e, :], start=True, stop=False)
                            mm = t_.matmul(y, ones[0:1, :], b2[:, e, :], start=False, stop=True)
                        mm.then_inc(S["g_ymm"], 1)
                        if e + 1 < NE:
                            hidden(b, e + 1)

                sequence(0)
                with pe.Fori(1, NB) as b:
                    sequence(b)


def attention(nc, k, a):
    x, h_all, ident, mod, lg, bank, S = k.x, k.h_all, k.ident, k.mod, k.lg, k.bank, k.S
    wait, alone = k.wait, k.alone
    k.sems(("a_set", "l_in", "q_queued", "q_filled"), counting_on=("a_stats", "a_mv", "a_ve", "a_rs", "a_xn", "a_t", "a_h",
            "q_mm", "k_mm", "v_mm", "q_ev", "k_ev", "v_ev", "wo_g", "bog", "bo_x",
            "sc_mm", "sc_max", "sc_exp", "p_t", "p_ev", "p_rinv", "ot_mm", "ot_ev", "op_mm", "op_x",
            "b_stats", "b_mv", "b_ve", "b_rs", "b_xn", "b_t", "b_h", "b_lg_mm", "b_lg",
            "b_scaled", "b_row", "b_rows", "q_max", "q_at", "q_best", "q_diff", "q_mask", "q_ms", "q_exp", "q_rank", "q_pos", "q_dest", "q_step"))
    with ExitStack() as ctx:
        sb = lambda name, shape, dt=F32: ctx.enter_context(nc.sbuf_tensor(name, shape, dt))
        st_a = sb("st_a", [P, NC, 6]); mv_a = sb("mv_a", [P, NC, 2]); ve_a = sb("ve_a", [P, NC]); rs_a = sb("rs_a", [P, NC])
        st_b = sb("st_b", [P, NC, 6]); mv_b = sb("mv_b", [P, NC, 2]); ve_b = sb("ve_b", [P, NC]); rs_b = sb("rs_b", [P, NC])
        xn_a = sb("xn_a", [P, NC, D]); xn_b = sb("xn_b", [P, NC, D])
        h3 = sb("h3", [P, SEQ]); h4 = sb("h4", [P, SEQ])
        bq = sb("bq", [P, 1])
        wog = sb("wog", [P, D])
        bog = sb("bog", [P, D])
        qT = sb("qT", [P, SEQ]); kT = sb("kT", [P, SEQ]); vv = sb("vv", [P, NC, D])
        nmx = sb("nmx", [P, NC]); sm = sb("sm", [P, NC]); rinv = sb("rinv", [P, NC])
        pr = sb("pr", [P, NC, SEQ]); pt = sb("pt", [P, NC, SEQ])
        oT = sb("oT", [P, SEQ])
        lg4 = sb("lg4", [P, NC, NE]); top = sb("top", [P, NC, NE]); top_i = sb("top_i", [P, NC, NE], U32); topf = sb("topf", [P, NC, 2])
        ediff = sb("ediff", [P, NC]); mk = sb("mk", [P, 2, NC, NE]); ms = sb("ms", [P, NC, NE]); rk = sb("rk", [P, NC, NE]); base = sb("base", [P, NC + 1, NE])
        mr = sb("mr", [P, 2, NC, NE]); posf = sb("posf", [P, 2, NC]); pos = sb("pos", [P, 2, NC], I32); wa = sb("wa", [P, NC])
        row = sb("row", [P, NC, 2, ROW]); scaled = sb("scaled", [P, NC, D])
        dest = sb("dest", [P, NT, 2], I32); tri = sb("tri", [P, P])
        h4_rows = h_all[:].rearrange("p b (c d) -> p (b c) d", c=NC)
        wq, wk, wv, wo = (k.attn_w[:, i, :] for i in range(4))
        block = ctx.enter_context(nc.Block())

        def run(e, body):
            body(-1, True, False, False, False)
            body(0, True, True, False, False)
            body(1, True, True, True, False)
            body(2, True, True, True, True)
            with e.Fori(3, NB - 1) as s:
                body(s, True, True, True, True)
            body(NB - 1, False, True, True, True)
            body(NB, False, False, True, True)
            body(NB + 1, False, False, False, True)

        def rows(s):
            return bass.ds(s * NC, NC)

        @block.sync
        def _(sp):
            for dst, key in ((dest[:], "dest"), (tri[:], "tri"), (k.filled[:], "queue_starts")):
                sp.dma_start(dst, a[key]).then_inc(S["l_in"], 16)
            sp.wait_ge(S["l_in"], 48)
            for dst, key in ((k.gamma, "gamma"), (k.beta, "beta"), (k.pad_rows, "pad_rows"), (k.starts, "queue_starts"), (k.tile_rows, "tile_rows"), (k.pad_at, "pad_at"),
                             (k.w1, "w1"), (k.b1, "b1"), (k.w2, "w2"), (k.b2, "b2")):
                sp.dma_start(dst[:], a[key]).then_inc(S["l_in"], 16)
            sp.wait_ge(S["l_in"], 16 * 13)
            sp.dma_start(k.queue[NE * REGION:, :].rearrange("(e p) r -> p e r", p=P), k.pad_rows[:, NE:, :]).then_inc(S["l_in"], 16)
            sp.wait_ge(S["l_in"], 16 * 14)

        @block.gpsimd
        def _(pool):
            g = nc.gpsimd
            g.memset(row[:], 0.0)
            g.tensor_scalar(bq[:], k.attn_b[:, 0:1], 0.125, None, ALU.mult).then_inc(S["a_set"], 1)
            pool.wait_ge(S["a_set"], 1)

            def body(s, A, B, C, Q):
                if A:
                    wait(pool, "a_mv", NC * (s + 2))
                    g.tensor_tensor(ve_a[:], mv_a[:].rearrange("p c t -> p (c t)")[:, 1::2], k.eps[:], ALU.add).then_inc(S["a_ve"], 1)
                    wait(pool, "a_ve", s + 2)
                    g.tensor_tensor(rs_a[:], ve_a[:], k.half_neg[:], ALU.pow).then_inc(S["a_rs"], 1)
                if B:
                    wait(pool, "bo_x", s)
                    alone(pool, s)
                    g.tensor_tensor(bog[:], k.bo[:], k.gate_rows[:, 1, s, :], ALU.mult).then_inc(S["bog"], 1)
                    wait(pool, "bog", s + 1)
                    wait(pool, "a_xn", NC * (s + 1))
                    alone(pool, s)
                    g.tensor_tensor(x[:, rows(s), :], x[:, rows(s), :], bog[:].rearrange("p (o d) -> p o d", o=1).broadcast_to([P, NC, D]),
                                    ALU.add).then_inc(S["bo_x"], 1)
                    wait(pool, "op_mm", s)
                    alone(pool, s)
                    g.tensor_tensor(wog[:], wo, k.gate_rows[:, 1, s, :], ALU.mult).then_inc(S["wo_g"], 1)
                if C:
                    wait(pool, "b_mv", NC * s)
                    g.tensor_tensor(ve_b[:], mv_b[:].rearrange("p c t -> p (c t)")[:, 1::2], k.eps[:], ALU.add).then_inc(S["b_ve"], 1)
                    wait(pool, "b_ve", s)
                    g.tensor_tensor(rs_b[:], ve_b[:], k.half_neg[:], ALU.pow).then_inc(S["b_rs"], 1)
                if Q:
                    wait(pool, "q_pos", s - 1)
                    wait(pool, "q_dest", s - 1)
                    wait(pool, "b_rows", s - 1)
                    alone(pool, s)
                    for c in range(NC):
                        for i in range(2):
                            pool.indirect_dma_start(k.queue, bass.IndirectOffsetOnAxis(ap=pos[:, i, c:c + 1], axis=0),
                                                    row[:, c, i, :], None).then_inc(S["q_queued"], 16)
                if C:
                    wait(pool, "b_xn", NC * s)
                    alone(pool, s)
                    g.tensor_tensor(scaled[:], xn_b[:], k.moe_rows[:, s - 1, 1, :].rearrange("p (o d) -> p o d", o=1).broadcast_to([P, NC, D]),
                                    ALU.mult).then_inc(S["b_scaled"], 1)
                    wait(pool, "b_scaled", s)
                    wait(pool, "q_queued", 16 * 2 * NC * (s - 1))
                    alone(pool, s)
                    g.tensor_tensor(row[:, :, 0, 0:D], scaled[:], k.moe_rows[:, s - 1, 0, :].rearrange("p (o d) -> p o d", o=1).broadcast_to([P, NC, D]),
                                    ALU.add).then_inc(S["b_row"], 1)

            run(pool, body)

        @block.scalar
        def _(act):
            ac = nc.scalar
            act.wait_ge(S["a_set"], 1)

            def body(s, A, B, C, Q):
                if Q:
                    wait(act, "q_diff", s - 1)
                    ac.activation(ediff[:], ediff[:], ACT.Exp).then_inc(S["q_exp"], 1)
                if C:
                    wait(act, "ot_mm", s)
                    ac.activation(oT[:], bank[0][:], ACT.Copy).then_inc(S["ot_ev"], 1)
                if B:
                    wait(act, "q_mm", s + 1)
                    ac.activation(qT[:], bank[1][:], ACT.Identity, scale=0.125, bias=bq[:]).then_inc(S["q_ev"], 1)
                    wait(act, "k_mm", s + 1)
                    ac.activation(kT[:], bank[2][:], ACT.Identity, bias=k.attn_b[:, 1:2]).then_inc(S["k_ev"], 1)
                if Q:
                    wait(act, "b_row", s - 1)
                    alone(act, s)
                    ac.activation(row[:, :, 1, 0:D], row[:, :, 0, 0:D], ACT.Copy)
                    ac.activation(h4_rows[:, rows(s - 2), :], row[:, :, 0, 0:D], ACT.Copy).then_inc(S["b_rows"], 1)
                for c in range(NC):
                    if B:
                        wait(act, "sc_max", NC * s + c + 1)
                        ac.activation(pr[:, c, :], bank[5 + c % 2][:], ACT.Exp, bias=nmx[:, c:c + 1], accum_out=sm[:, c:c + 1]).then_inc(S["sc_exp"], 1)
                    if A and c == 1:
                        wait(act, "a_t", s + 2)
                        alone(act, s)
                        ac.activation(h3[:], bank[0][:], ACT.Identity, scale=mod[:, 1, 1, bass.ds(s + 1, 1)],
                                      bias=mod[:, 1, 0, bass.ds(s + 1, 1)]).then_inc(S["a_h"], 1)
                if C:
                    wait(act, "b_t", s)
                    alone(act, s)
                    ac.activation(h4[:], bank[1][:], ACT.Identity, scale=mod[:, 1, 4, bass.ds(s - 1, 1)],
                                  bias=mod[:, 1, 3, bass.ds(s - 1, 1)]).then_inc(S["b_h"], 1)

            run(act, body)

        @block.vector
        def _(dve):
            v = nc.vector
            dve.wait_ge(S["l_in"], 48)
            dve.wait_ge(S["a_set"], 1)
            v.tensor_copy(base[:, 0, :], k.filled[:])

            def body(s, A, B, C, Q):
                if A:
                    for c in range(NC):
                        v.bn_stats(st_a[:, c, :], x[:, (s + 1) * NC + c, :]).then_inc(S["a_stats"], 1)
                    wait(dve, "a_rs", s + 1)
                    wait(dve, "a_stats", NC * (s + 2))
                    alone(dve, s)
                    for c in range(NC):
                        v.bn_aggr(mv_a[:, c, :], st_a[:, c, :]).then_inc(S["a_mv"], 1)
                if B:
                    wait(dve, "v_mm", s + 1)
                    v.tensor_tensor(vv[:], bank[3][:].rearrange("p (c d) -> p c d", c=NC),
                                    k.bv[:].rearrange("p (o d) -> p o d", o=1).broadcast_to([P, NC, D]), ALU.add).then_inc(S["v_ev"], 1)
                if C:
                    wait(dve, "op_mm", s)
                    wait(dve, "bo_x", s)
                    wait(dve, "p_rinv", s)
                    for c in range(NC):
                        v.scalar_tensor_tensor(out=x[:, (s - 1) * NC + c, :], in0=bank[4][:, c * P:c * P + P], scalar=rinv[:, c:c + 1],
                                               in1=x[:, (s - 1) * NC + c, :], op0=ALU.mult, op1=ALU.add).then_inc(S["op_x"], 1)
                    wait(dve, "op_x", NC * s)
                    alone(dve, s)
                    for c in range(NC):
                        v.bn_stats(st_b[:, c, :], x[:, (s - 1) * NC + c, :]).then_inc(S["b_stats"], 1)
                    wait(dve, "b_stats", NC * s)
                    wait(dve, "b_xn", NC * (s - 1))
                    alone(dve, s)
                    for c in range(NC):
                        v.bn_aggr(mv_b[:, c, :], st_b[:, c, :]).then_inc(S["b_mv"], 1)
                for c in range(NC):
                    if B:
                        wait(dve, "sc_mm", NC * s + c + 1)
                        alone(dve, s)
                        v.tensor_reduce(nmx[:, c:c + 1], bank[5 + c % 2][:], AX.X, ALU.max, negate=True).then_inc(S["sc_max"], 1)
                    if A and c == 1:
                        wait(dve, "a_rs", s + 2)
                        wait(dve, "a_t", s + 1)
                        for c2 in range(NC):
                            v.tensor_scalar(xn_a[:, c2, :], x[:, (s + 1) * NC + c2, :], mv_a[:, c2, 0:1], rs_a[:, c2:c2 + 1],
                                            ALU.subtract, ALU.mult).then_inc(S["a_xn"], 1)
                    if C and c == 1:
                        wait(dve, "b_rs", s)
                        wait(dve, "b_t", s - 1)
                        for c2 in range(NC):
                            v.tensor_scalar(xn_b[:, c2, :], x[:, (s - 1) * NC + c2, :], mv_b[:, c2, 0:1], rs_b[:, c2:c2 + 1],
                                            ALU.subtract, ALU.mult).then_inc(S["b_xn"], 1)
                if B:
                    for c in range(NC):
                        wait(dve, "p_t", NC * s + c + 1)
                        v.tensor_copy(pt[:, :, c * P:c * P + P], bank[7 if c % 2 == 0 else 3][:].rearrange("p (k q) -> p k q", k=NC)).then_inc(S["p_ev"], 1)
                    wait(dve, "op_x", NC * s)
                    alone(dve, s)
                    v.reciprocal(rinv[:], sm[:]).then_inc(S["p_rinv"], 1)
                if Q:
                    n = [9 * (s - 2)]

                    def step(ins):
                        n[0] = n[0] + 1
                        ins.then_inc(S["q_step"], 1)
                        wait(dve, "q_step", n[0])

                    wait(dve, "q_rank", s - 1)
                    for c in range(NC):
                        step(v.tensor_tensor(base[:, c + 1, :], bank[2][:, 96 + c * NE:96 + c * NE + NE], base[:, c, :], ALU.add))
                    step(v.tensor_tensor(rk[:], bank[2][:, 64:64 + NC * NE].rearrange("p (c e) -> p c e", c=NC), base[:, 0:NC, :], ALU.add))
                    step(v.tensor_copy(base[:, 0, :], base[:, NC, :]))
                    step(v.tensor_tensor(mr[:].rearrange("p i c e -> p i (c e)"), mk[:].rearrange("p i c e -> p i (c e)"),
                                         rk[:].rearrange("p (o c) e -> p o (c e)", o=1).broadcast_to([P, 2, NC * NE]), ALU.mult))
                    step(v.tensor_reduce(posf[:], mr[:], AX.X, ALU.add))
                    wait(dve, "q_queued", 16 * 2 * NC * (s - 2))
                    v.tensor_copy(pos[:], posf[:]).then_inc(S["q_pos"], 1)
                    v.tensor_copy(row[:, :, :, D:D + 1].bitcast(I32), dest[:, rows(s - 2), :].rearrange("p c (i o) -> p c i o", o=1)).then_inc(S["q_dest"], 1)
                    wait(dve, "q_exp", s - 1)
                    v.tensor_scalar(wa[:], ediff[:], 1.0, None, ALU.add).then_inc(S["q_best"], 1)
                    wait(dve, "q_best", 2 * (s - 2) + 1)
                    v.reciprocal(k.top_w[:, 0, rows(s - 2)], wa[:]).then_inc(S["q_best"], 1)
                    wait(dve, "q_best", 2 * (s - 2) + 2)
                    step(v.tensor_tensor(k.top_w[:, 1, rows(s - 2)], k.top_w[:, 0, rows(s - 2)], ediff[:], ALU.mult))
                if C:
                    wait(dve, "b_lg_mm", s)
                    alone(dve, s)
                    v.tensor_tensor(lg4[:], bank[2][:, 0:NC * NE].rearrange("p (c e) -> p c e", c=NC),
                                    k.br[:].rearrange("p (o e) -> p o e", o=1).broadcast_to([P, NC, NE]), ALU.add).then_inc(S["b_lg"], 1)
                    wait(dve, "b_lg", s)
                    alone(dve, s)
                    for c in range(NC):
                        v.max(top[:, c, :], lg4[:, c, :]).then_inc(S["q_max"], 1)
                    wait(dve, "q_max", NC * s)
                    alone(dve, s)
                    for c in range(NC):
                        v.max_index(top_i[:, c, :], top[:, c, :], lg4[:, c, :]).then_inc(S["q_at"], 1)
                    v.tensor_tensor(ediff[:].rearrange("p (c o) -> p c o", o=1), top[:, :, 1:2], top[:, :, 0:1], ALU.subtract).then_inc(S["q_diff"], 1)
                    wait(dve, "q_at", NC * s)
                    alone(dve, s)
                    v.tensor_copy(topf[:], top_i[:, :, 0:2]).then_inc(S["q_mask"], 1)
                    wait(dve, "q_mask", 3 * (s - 1) + 1)
                    for i in range(2):
                        v.tensor_tensor(mk[:, i], topf[:, :, i:i + 1].broadcast_to([P, NC, NE]),
                                        k.iota[:].rearrange("p (o e) -> p o e", o=1).broadcast_to([P, NC, NE]), ALU.is_equal).then_inc(S["q_mask"], 1)
                    wait(dve, "q_mask", 3 * s)
                    v.tensor_tensor(ms[:], mk[:, 0], mk[:, 1], ALU.add).then_inc(S["q_ms"], 1)

            run(dve, body)
            v.tensor_copy(k.filled[:], base[:, 0, :]).then_inc(S["q_filled"], 1)
            dve.wait_ge(S["q_filled"], 1)

        @block.tensor
        def _(pe):
            t_ = nc.tensor
            pe.wait_ge(S["l_in"], 48)

            def body(s, A, B, C, Q):
                if C:
                    wait(pe, "p_ev", NC * s)
                    wait(pe, "a_h", s + 1 if A or B else NB)
                    for i in range(NC):
                        mm = t_.matmul(bank[0][:], vv[:, i, :], pt[:, i, :], start=(i == 0), stop=(i == NC - 1))
                    mm.then_inc(S["ot_mm"], 1)
                if B:
                    wait(pe, "a_h", s + 1)
                    wait(pe, "b_h", s - 1)
                    t_.matmul(bank[1][:], wq, h3[:], start=True, stop=True).then_inc(S["q_mm"], 1)
                    wait(pe, "b_lg", s - 1)
                    wait(pe, "q_step", 9 * (s - 2))
                    t_.matmul(bank[2][:], wk, h3[:], start=True, stop=True).then_inc(S["k_mm"], 1)
                    wait(pe, "p_ev", NC * s)
                    for c in range(NC):
                        mm = t_.matmul(bank[3][:, c * P:c * P + P], h3[:, c * P:c * P + P], wv, start=True, stop=True)
                    mm.then_inc(S["v_mm"], 1)
                if C:
                    wait(pe, "ot_ev", s)
                    wait(pe, "wo_g", s)
                    wait(pe, "op_x", NC * (s - 1))
                    for c in range(NC):
                        mm = t_.matmul(bank[4][:, c * P:c * P + P], oT[:, c * P:c * P + P], wog[:], start=True, stop=True)
                    mm.then_inc(S["op_mm"], 1)
                if B:
                    wait(pe, "q_ev", s + 1)
                    wait(pe, "k_ev", s + 1)
                    for c in range(NC):
                        wait(pe, "sc_exp", NC * s + c - 1)
                        t_.matmul(bank[5 + c % 2][:], qT[:, c * P:c * P + P], kT[:], start=True, stop=True).then_inc(S["sc_mm"], 1)
                if A:
                    wait(pe, "ot_ev", s)
                    wait(pe, "a_h", s + 1)
                    wait(pe, "a_xn", NC * (s + 2))
                    for c in range(NC):
                        mm = t_.transpose(bank[0][:, c * P:c * P + P], xn_a[:, c, :], ident[:])
                    mm.then_inc(S["a_t"], 1)
                if Q:
                    wait(pe, "q_ms", s - 1)
                    wait(pe, "k_ev", s + 1 if B else NB)
                    wait(pe, "b_lg", s - 1)
                    t_.matmul(bank[2][:, 64:64 + NC * NE], tri[:], ms[:].rearrange("p c e -> p (c e)"), start=True, stop=True)
                    t_.matmul(bank[2][:, 96:96 + NC * NE], k.ones[:], ms[:].rearrange("p c e -> p (c e)"), start=True, stop=True).then_inc(S["q_rank"], 1)
                if B:
                    for c in range(NC):
                        wait(pe, "sc_exp", NC * s + c + 1)
                        wait(pe, "p_ev", NC * s + c - 1)
                        if c == 1:
                            wait(pe, "v_ev", s + 1)
                        for i in range(NC):
                            mm = t_.transpose(bank[7 if c % 2 == 0 else 3][:, i * P:i * P + P], pr[:, c, i * P:i * P + P], ident[:])
                        mm.then_inc(S["p_t"], 1)
                if C:
                    wait(pe, "b_xn", NC * s)
                    wait(pe, "q_ev", s + 1 if B else NB)
                    for c in range(NC):
                        mm = t_.transpose(bank[1][:, c * P:c * P + P], xn_b[:, c, :], ident[:])
                    mm.then_inc(S["b_t"], 1)
                    wait(pe, "b_h", s)
                    wait(pe, "k_ev", s + 1 if B else NB)
                    if Q:
                        wait(pe, "q_step", 9 * (s - 2) + 6)
                    for c in range(NC):
                        mm = t_.matmul(bank[2][:, c * NE:c * NE + NE], h4[:, c * P:c * P + P], k.wr[:], start=True, stop=True)
                    mm.then_inc(S["b_lg_mm"], 1)

            run(pe, body)


def l1_experts(nc, k, a, out):
    x, ident, bank, S, filled, w1, w2, b1, b2 = k.x, k.ident, k.bank, k.S, k.filled, k.w1, k.w2, k.b1, k.b2
    wait, alone = k.wait, k.alone
    UN = 8
    k.sems(("e_step", "e_tab", "e_pad", "e_pads", "e_out")
           + tuple(f"tile_in{i}" for i in range(UN)) + tuple(f"y_out{i}" for i in range(UN)) + ("y_in0", "y_in1"),
           counting_on=("x_t", "x_ev", "h_mm", "h_ev", "ht_mm", "ht_ev", "y_mm", "y_ev",
            "s_1", "s_2", "f_stats", "f_mv", "f_ve", "f_rs", "f_n", "f_x", "f_gg", "f_g", "f_x2"))
    h4_rows = k.h_all[:].rearrange("p b (c d) -> p (b c) d", c=NC)
    with ExitStack() as ctx:
        sb = lambda name, shape, dt=F32: ctx.enter_context(nc.sbuf_tensor(name, shape, dt))
        starts, tile_rows, pad_at, pad_rows, gg, gb = k.starts, k.tile_rows, k.pad_at, k.pad_rows, k.gg, k.gb
        count = sb("count", [P, NE]); over = sb("over", [P, NE, NT]); tiles = sb("tiles", [P, NE]); ends = sb("ends", [P, NE])
        skip = sb("skip", [P, NE]); past = sb("past", [P, TILES, NE]); tile_f = sb("tile_f", [P, TILES]); tile_e = sb("tile_e", [P, TILES], I32)
        tile_r = sb("tile_r", [P, TILES]); tile_at = sb("tile_at", [P, TILES], I32)
        padf = sb("padf", [P, NE]); padi = sb("padi", [P, NE], I32)
        xg = sb("xg", [P, UN, ROW]); xt = sb("xt", [P, 2, P]); hs = sb("hs", [P, 2, FF]); ht = sb("ht", [P, 2, FF]); ys = sb("ys", [P, UN, D])
        yy = sb("yy", [P, 2, 2, NC, D]); acc = sb("acc", [P, NC, D]); tgt = sb("tgt", [P, 2, NC, D])
        st = sb("st_f", [P, NC, 6]); mv = sb("mv_f", [P, 2, NC, 2]); ve = sb("ve_f", [P, NC]); rs = sb("rs_f", [P, 2, NC])
        nn = sb("nn", [P, NC, D]); ng = sb("ng", [P, NC, D])
        block = ctx.enter_context(nc.Block())

        def rounds(e, body):
            for s in range(-2, UN):
                body(s, s % UN, s // UN, lambda lag: 0 <= s - lag < TILES)
            with e.Fori(1, TILES // UN - 1) as i:
                for c in range(UN):
                    body(i * UN + c, c, i, lambda lag: True)
            for s in range(TILES - UN, TILES + 1):
                body(s, s % UN, s // UN, lambda lag: 0 <= s - lag < TILES)

        def expert(e, t):
            at = tile_e[0:1, t:t + 1] if isinstance(t, int) else tile_e[0:1, bass.ds(t, 1)]
            return e.value_load(at, min_val=0, max_val=NE - 1)

        @block.sync
        def _(sp):
            sp.wait_ge(S["e_tab"], 1)
            sp.wait_ge(S["q_queued"], 16 * 2 * NT)
            sp.wait_ge(S["e_pads"], 16 * NE)

            def load(t, c, rnd):
                wait(sp, f"y_out{c}", 16 * rnd)
                at = tile_at[0:1, t:t + 1] if isinstance(t, int) else tile_at[0:1, bass.ds(t, 1)]
                r = sp.value_load(at, min_val=0, max_val=(NE * REGION + NE * P) - P)
                sp.dma_start(xg[:, c, :], k.queue[bass.ds(r, P), :]).then_inc(S[f"tile_in{c}"], 16)

            for c in range(UN):
                load(c, c, 0)
            with sp.Fori(1, TILES // UN) as i:
                for c in range(UN):
                    load(i * UN + c, c, i)
            for c in range(UN):
                sp.wait_ge(S[f"y_out{c}"], 16 * (TILES // UN))
            rv = k.results[0:2 * NTOK, :].rearrange("(i t p) d -> p i t d", i=2, p=P)
            ov = out.rearrange("b (c p) d -> p (b c) d", p=P)

            def bring(b, par, rnd):
                wait(sp, "s_2", NC * (b - 1))
                for i in range(2):
                    sp.dma_start(yy[:, par, i], rv[:, i, bass.ds(b * NC, NC), :]).then_inc(S[f"y_in{par}"], 16)

            def send(b):
                wait(sp, "f_x2", b + 1)
                sp.dma_start(ov[:, bass.ds(b * NC, NC), :], x[:, bass.ds(b * NC, NC), :]).then_inc(S["e_out"], 16)

            bring(0, 0, 0)
            bring(1, 1, 0)
            with sp.Fori(1, NB // 2) as i:
                for par in range(2):
                    bring(2 * i + par, par, i)
                    send(2 * i + par - 2)
            send(NB - 2)
            send(NB - 1)
            sp.wait_ge(S["e_out"], 16 * NB)

        @block.gpsimd
        def _(pool):
            g = nc.gpsimd
            pool.wait_ge(S["e_pad"], 1)
            for e in range(NE):
                pool.indirect_dma_start(k.queue, bass.IndirectOffsetOnAxis(ap=padi[:, e:e + 1], axis=0), pad_rows[:, e, :], None).then_inc(S["e_pads"], 16)
            def tile(s, c, i, has):
                if has(1):
                    cc = (c - 1) % UN
                    wait(pool, "y_ev", s)
                    alone(pool, s)
                    pool.indirect_dma_start(k.results, bass.IndirectOffsetOnAxis(ap=xg[:, cc, D:D + 1].bitcast(I32), axis=0),
                                            ys[:, cc, :], None).then_inc(S[f"y_out{cc}"], 16)
                if c == 1 and (not isinstance(s, int) or 0 <= i < NB):
                    g.tensor_tensor(gg[:, i, :], k.gamma[:], k.gate_rows[:, 2, i, :], ALU.mult)
                    g.tensor_tensor(gb[:, i, :], k.beta[:], k.gate_rows[:, 2, i, :], ALU.mult).then_inc(S["f_gg"], 1)
                if c == UN // 2 and (not isinstance(s, int) or 0 <= i < NB):
                    wait(pool, "f_gg", i + 1)
                    alone(pool, s)
                    g.tensor_tensor(x[:, bass.ds(i * NC, NC), :], x[:, bass.ds(i * NC, NC), :],
                                    gb[:, i, :].rearrange("p (o d) -> p o d", o=1).broadcast_to([P, NC, D]), ALU.add).then_inc(S["f_x"], 1)

            rounds(pool, tile)

            pool.wait_ge(S["f_x"], NB)

            def scale(i, par):
                b = 2 * i + par
                wait(pool, "f_mv", NC * (b + 1))
                wait(pool, "f_rs", b)
                wait(pool, "f_n", b - 1)
                g.tensor_tensor(ve[:], mv[:, par].rearrange("p c t -> p (c t)")[:, 1::2], k.eps[:], ALU.add).then_inc(S["f_ve"], 1)
                wait(pool, "f_ve", b + 1)
                g.tensor_tensor(rs[:, par, :], ve[:], k.half_neg[:], ALU.pow).then_inc(S["f_rs"], 1)

            def join(i, par):
                b = 2 * i + par
                wait(pool, "f_n", b + 1)
                wait(pool, "f_x2", b)
                alone(pool, i)
                g.tensor_tensor(ng[:], nn[:], gg[:, b, :].rearrange("p (o d) -> p o d", o=1).broadcast_to([P, NC, D]), ALU.mult).then_inc(S["f_g"], 1)
                wait(pool, "f_g", b + 1)
                alone(pool, i)
                g.tensor_tensor(x[:, bass.ds(b * NC, NC), :], x[:, bass.ds(b * NC, NC), :], ng[:], ALU.add).then_inc(S["f_x2"], 1)

            scale(0, 0)
            scale(0, 1)
            join(0, 0)
            with pool.Fori(1, NB // 2) as i:
                scale(i, 0)
                join(i - 1, 1)
                scale(i, 1)
                join(i, 0)
            join(NB // 2 - 1, 1)

        @block.scalar
        def _(act):
            ac = nc.scalar

            def tile(s, c, i, has):
                p = c % 2
                if has(-2):
                    wait(act, "x_t", s + 3)
                    wait(act, "h_mm", s + 1)
                    ac.activation(xt[:, p, :], bank[p][:, 0:P], ACT.Copy).then_inc(S["x_ev"], 1)
                if has(0):
                    wait(act, "ht_mm", s + 1)
                    wait(act, "y_mm", s - 1)
                    ac.activation(ht[:, p, :], bank[4 + p][:], ACT.Relu).then_inc(S["ht_ev"], 1)

            rounds(act, tile)

        @block.vector
        def _(dve):
            v = nc.vector
            n = [0]

            def step(ins):
                n[0] += 1
                ins.then_inc(S["e_step"], 1)
                dve.wait_ge(S["e_step"], n[0])

            row = lambda ap, m: ap.rearrange("p (o e) -> p o e", o=1).broadcast_to([P, m, NE])
            step(v.tensor_scalar(padf[:], filled[:], pad_at[:], None, ALU.add))
            v.tensor_copy(padi[:], padf[:]).then_inc(S["e_pad"], 1)
            step(v.tensor_tensor(count[:], filled[:], starts[:], ALU.subtract))
            step(v.tensor_tensor(over[:], bc3(count[:], NE, NT),
                                 tile_rows[:, 0:NT].rearrange("p (o t) -> p o t", o=1).broadcast_to([P, NE, NT]), ALU.is_gt))
            step(v.tensor_reduce(tiles[:], over[:], AX.X, ALU.add))
            step(v.tensor_tensor_scan(ends[:], k.ones[:, 0:NE], tiles[:], 0.0, ALU.mult, ALU.add))
            step(v.tensor_scalar(skip[:], tiles[:], -float(P), float(REGION), ALU.mult, ALU.add))
            step(v.tensor_scalar(ends[:], ends[:], float(P), None, ALU.mult))
            step(v.tensor_tensor(past[:], bc3(tile_rows[:], TILES, NE), row(ends[:], TILES), ALU.is_ge))
            step(v.tensor_reduce(tile_f[:], past[:], AX.X, ALU.add))
            step(v.tensor_scalar(tile_f[:], tile_f[:], float(NE - 1), None, ALU.min))
            step(v.tensor_copy(tile_e[:], tile_f[:]))
            step(v.tensor_tensor(past[:], past[:], row(skip[:], TILES), ALU.mult))
            step(v.tensor_reduce(tile_r[:], past[:], AX.X, ALU.add))
            step(v.tensor_tensor(tile_r[:], tile_r[:], tile_rows[:], ALU.add))
            v.tensor_copy(tile_at[:], tile_r[:]).then_inc(S["e_tab"], 1)
            dve.wait_ge(S["e_tab"], 1)

            def tile(s, c, i, has):
                p = c % 2
                if has(-1):
                    e = expert(dve, s + 1)
                    wait(dve, "h_mm", s + 2)
                    wait(dve, "ht_mm", s)
                    v.tensor_tensor(hs[:, 1 - p, :], bank[3 - p][:], b1[:, e, :], ALU.add).then_inc(S["h_ev"], 1)
                if has(1):
                    e = expert(dve, s - 1)
                    wait(dve, "y_mm", s)
                    cc = (c - 1) % UN
                    wait(dve, f"y_out{cc}", 16 * (i if c else i - 1))
                    alone(dve, s)
                    v.tensor_tensor(ys[:, cc, :], bank[7 - p][:, 0:D], b2[:, e, :], ALU.add).then_inc(S["y_ev"], 1)

            rounds(dve, tile)

            def gather(i, par):
                b = 2 * i + par
                wait(dve, f"y_in{par}", 32 * (i + 1))
                wait(dve, "s_2", NC * b)
                for c in range(NC):
                    v.scalar_tensor_tensor(out=acc[:, c, :], in0=yy[:, par, 0, c, :], scalar=k.top_w[:, 0, bass.ds(b * NC + c, 1)],
                                           in1=h4_rows[:, b * NC + c, :], op0=ALU.mult, op1=ALU.add).then_inc(S["s_1"], 1)
                wait(dve, "s_1", NC * (b + 1))
                wait(dve, "f_n", b - 1)
                for c in range(NC):
                    v.scalar_tensor_tensor(out=tgt[:, par, c, :], in0=yy[:, par, 1, c, :], scalar=k.top_w[:, 1, bass.ds(b * NC + c, 1)],
                                           in1=acc[:, c, :], op0=ALU.mult, op1=ALU.add).then_inc(S["s_2"], 1)
                wait(dve, "s_2", NC * (b + 1))
                wait(dve, "f_mv", NC * b)
                alone(dve, i)
                for c in range(NC):
                    v.bn_stats(st[:, c, :], tgt[:, par, c, :]).then_inc(S["f_stats"], 1)
                wait(dve, "f_stats", NC * (b + 1))
                alone(dve, i)
                for c in range(NC):
                    v.bn_aggr(mv[:, par, c, :], st[:, c, :]).then_inc(S["f_mv"], 1)

            def norm(i, par):
                b = 2 * i + par
                wait(dve, "f_rs", b + 1)
                wait(dve, "f_g", b)
                for c in range(NC):
                    ins = v.tensor_scalar(nn[:, c, :], tgt[:, par, c, :], mv[:, par, c, 0:1], rs[:, par, c:c + 1], ALU.subtract, ALU.mult)
                ins.then_inc(S["f_n"], 1)

            gather(0, 0)
            gather(0, 1)
            norm(0, 0)
            with dve.Fori(1, NB // 2) as i:
                gather(i, 0)
                norm(i - 1, 1)
                gather(i, 1)
                norm(i, 0)
            norm(NB // 2 - 1, 1)

        @block.tensor
        def _(pe):
            t_ = nc.tensor
            pe.wait_ge(S["e_tab"], 1)

            def tile(s, c, i, has):
                p = c % 2
                if has(-2):
                    c2 = (c + 2) % UN
                    wait(pe, f"tile_in{c2}", 16 * (i + 1 if c < UN - 2 else i + 2))
                    wait(pe, "x_ev", s + 1)
                    t_.transpose(bank[p][:, 0:P], xg[:, c2, 0:D], ident[:]).then_inc(S["x_t"], 1)
                if has(-1):
                    e = expert(pe, s + 1)
                    wait(pe, "x_ev", s + 2)
                    wait(pe, "h_ev", s)
                    t_.matmul(bank[3 - p][:], xt[:, 1 - p, :], w1[:, e, :], start=True, stop=True).then_inc(S["h_mm"], 1)
                if has(0):
                    wait(pe, "h_ev", s + 1)
                    wait(pe, "ht_ev", s - 1)
                    for g in range(NG):
                        mm = t_.transpose(bank[4 + p][:, g * P:g * P + P], hs[:, p, g * P:g * P + P], ident[:])
                    mm.then_inc(S["ht_mm"], 1)
                if has(1):
                    e = expert(pe, s - 1)
                    wait(pe, "ht_ev", s)
                    wait(pe, "y_ev", s - 2)
                    for g in range(NG):
                        mm = t_.matmul(bank[7 - p][:, 0:D], ht[:, 1 - p, g * P:g * P + P], w2[:, e, g, :], start=(g == 0), stop=(g == NG - 1))
                    mm.then_inc(S["y_mm"], 1)

            rounds(pe, tile)


def build_program(nc, a, out):
    with ExitStack() as ctx:
        k = Chip(nc, a, ctx)
        mixer(nc, k, a)
        l0_experts(nc, k, a)
        with ExitStack() as weights:
            k.expert_weights(weights)
            attention(nc, k, a)
            l1_experts(nc, k, a, out)


def _layouts(i):
    import numpy as np
    f = lambda v: np.ascontiguousarray(v)
    rep = lambda v: np.ascontiguousarray(np.broadcast_to(v, (P,) + v.shape))
    w = i["L0_attn_in_proj_w"]
    eye = np.eye(P, dtype=np.float32)
    sel = np.zeros((16, 16, P), np.float32)
    for k in range(16):
        sel[k, k] = 1
    sel127 = np.zeros((P, P), np.float32)
    sel127[P - 1] = 1
    pick = np.zeros((NB, NB, P), np.float32)
    for b in range(NB):
        pick[b, b] = 1
    tok = np.arange(NT)[None, :, None] * P + np.arange(P)[:, None, None] + np.arange(2)[None, None, :] * NTOK
    pad = np.zeros((P, 2 * NE, ROW), np.int32)
    pad[:, :, D] = 2 * NTOK + np.arange(2 * NE)[None, :] * P + np.arange(P)[:, None]
    return {
        "x": f(i["L0_attn_x"]),
        "cT": f(np.concatenate([i["L0_c"].T, i["L1_c"].T], 1)),
        "wmod": f(np.stack([i["L0_wmod"], i["L1_wmod"]], 1)),
        "w_xbc": f(w[DI:DI + 512].T),
        "w_zdt": f(np.concatenate([w[:DI], w[DI + 512:]]).T),
        "conv_w": rep(i["L0_attn_conv_w"].T),
        "conv_b": f(i["L0_attn_conv_b"].reshape(4, P).T),
        "dt_b": rep(i["L0_attn_dt_bias"]),
        "a_log": rep(np.tile(i["L0_attn_A_log"], NC)),
        "d_bc": rep(np.repeat(i["L0_attn_D"], HD)),
        "norm_w": f(i["L0_attn_norm_w"].reshape(2, P).T),
        "w_out": f(i["L0_attn_out_proj_w"].T.reshape(2, P, D).transpose(1, 0, 2)),
        "gate_w": f(i["L0_ffn_gate_w"].T),
        "ident": eye, "ident4": f(np.tile(eye, (1, NC))), "sel": f(sel.reshape(16, 16 * P)), "sel127": sel127,
        "iota": rep(np.arange(NE, dtype=np.float32)),
        "g_w1": f(i["L0_ffn_W1"].transpose(1, 0, 2)), "g_w2": f(i["L0_ffn_W2"].transpose(1, 0, 2)),
        "g_b1": f(i["L0_ffn_b1"].T), "g_b2": f(i["L0_ffn_b2"][None]),
        "pick": pick,
        "attn_w": f(np.stack([i[f"L1_attn_W{n}"].T for n in "qkvo"], 1)),
        "attn_b": f(np.stack([i["L1_attn_bq"], i["L1_attn_bk"]], 1)),
        "bv": rep(i["L1_attn_bv"]), "bo": rep(i["L1_attn_bo"]),
        "wr": f(i["L1_ffn_Wr"].T), "br": rep(i["L1_ffn_br"]),
        "w1": f(i["L1_ffn_W1"].transpose(2, 0, 1)),
        "b1": rep(i["L1_ffn_b1"]),
        "w2": f(i["L1_ffn_W2"].reshape(NE, D, NG, P).transpose(3, 0, 2, 1)),
        "b2": rep(i["L1_ffn_b2"]),
        "dest": f(tok.astype(np.int32)), "tri": f(np.triu(np.ones((P, P), np.float32), 1)),
        "queue_starts": rep(np.arange(NE, dtype=np.float32) * REGION),
        "tile_rows": rep(np.arange(TILES, dtype=np.float32) * P),
        "pad_at": f(np.arange(P, dtype=np.float32)[:, None]), "pad_rows": pad.view(np.float32),
        "gamma": rep(i["L1_ffn_gamma"]), "beta": rep(i["L1_ffn_beta"]),
    }


def kernel(**inputs):
    import numpy as _np
    import concourse.bacc as _bacc
    from concourse import mybir as _mybir
    from concourse.bass_utils import run_bass_kernel_spmd as _run

    nc = _bacc.Bacc("TRN2", target_bir_lowering=False, num_devices=1)
    arrays, args = {}, {}
    for name, v in _layouts({n: _np.asarray(v) for n, v in inputs.items()}).items():
        arrays["in_" + name] = v
        args[name] = nc.dram_tensor("in_" + name, v.shape, _mybir.dt.from_np(v.dtype), kind="ExternalInput").ap()
    out = nc.dram_tensor("out_x", (NB, SEQ, D), F32, kind="ExternalOutput").ap()
    build_program(nc, args, out)
    r = _run(nc, [arrays], core_ids=[0])
    return r.results[0]["out_x"]
```
